# Optimizing a Trainium2 kernel written in Bass

```python
import numpy as np
import jax
import jax.numpy as jnp

def _softmax(x, axis=-1):
    return jax.nn.softmax(x, axis=axis)

def _gelu(x):
    return jax.nn.gelu(x, approximate=True)

def _silu(x):
    return jax.nn.silu(x)

def _sigmoid(x):
    return jax.nn.sigmoid(x)

def _layernorm(x, axis=-1, eps=1e-05):
    m = jnp.mean(x, axis=axis, keepdims=True)
    v = jnp.var(x, axis=axis, keepdims=True)
    return (x - m) / jnp.sqrt(v + eps)

def _scatter_add(tgt, idx, src, axis=0):
    return tgt.at[idx].add(src)

def _segment_sum(src, seg, n):
    return jax.ops.segment_sum(src, seg, n)
kernel_name = 'mk_decoder_preln_d1_seqx_r4_14de15'

def setup_inputs(seed: int=0):
    np.random.seed(seed)
    _w = jnp.asarray

    def _rec_inputs():
        import jax
        import jax.numpy as jnp
        _rk = jax.random.key(seed)
        x = -0.0002928 + 1 * jax.random.normal(jax.random.fold_in(_rk, 1), (16, 256, 256), jnp.float32)
        _lenS = 256 - jax.random.randint(jax.random.fold_in(_rk, 7), (16,), 0, max(1, 256 // 4) + 1, jnp.int32)
        _lenS2 = 256 - jax.random.randint(jax.random.fold_in(_rk, 8), (16,), 0, max(1, 256 // 4) + 1, jnp.int32)
        _ctx_1024P = jax.random.normal(jax.random.fold_in(_rk, 11), (16, 16, 256), jnp.float32)
        _ctx_1024c = jax.random.dirichlet(jax.random.fold_in(_rk, 511), 0.3 * jnp.ones((16,), jnp.float32), (16, 256))
        _ctx_1024t = jnp.einsum('bsk,bkd->bsd', _ctx_1024c, _ctx_1024P)
        _ctx_1024t = _ctx_1024t * jax.lax.rsqrt(jnp.mean(jnp.square(_ctx_1024t)) + 1e-12) * 0.953939
        ctx_1024 = -1.39393e-06 + 0.999914 * (_ctx_1024t + 0.3 * jax.random.normal(jax.random.fold_in(_rk, 611), (16, 256, 256), jnp.float32))
        return (x, ctx_1024)
    x, ctx_1024 = _rec_inputs()

    def _L0_attn_setup():
        import jax, jax.numpy as jnp
        import numpy as np
        import math
        D_MODEL = 256
        N_HEADS = 16
        D_HEAD = D_MODEL // N_HEADS
        TOP_K = 64
        WM = 128
        IDX_DIM = 64
        B, S = (2, 512)
        key = jax.random.key(seed)
        ks = jax.random.split(key, 14)
        sc = 0.02
        inp = {'x': jax.random.normal(ks[0], (B, S, D_MODEL), dtype=jnp.float32), 'wq_w': jax.random.normal(ks[1], (D_MODEL, D_MODEL), dtype=jnp.float32) * sc, 'wq_b': jnp.zeros((D_MODEL,), jnp.float32), 'wk_w': jax.random.normal(ks[2], (D_MODEL, D_MODEL), dtype=jnp.float32) * sc, 'wk_b': jnp.zeros((D_MODEL,), jnp.float32), 'wv_w': jax.random.normal(ks[3], (D_MODEL, D_MODEL), dtype=jnp.float32) * sc, 'wv_b': jnp.zeros((D_MODEL,), jnp.float32), 'wo_w': jax.random.normal(ks[4], (D_MODEL, D_MODEL), dtype=jnp.float32) * sc, 'wo_b': jnp.zeros((D_MODEL,), jnp.float32), 'wqi_w': jax.random.normal(ks[5], (D_MODEL, IDX_DIM), dtype=jnp.float32) * sc, 'wqi_b': jnp.zeros((IDX_DIM,), jnp.float32), 'wki_w': jax.random.normal(ks[6], (D_MODEL, IDX_DIM), dtype=jnp.float32) * sc, 'wki_b': jnp.zeros((IDX_DIM,), jnp.float32)}
        return inp
    _L0_attn_all = _L0_attn_setup()
    _L0_attn_in = {k: v for k, v in _L0_attn_all.items() if k in ('wq_w', 'wq_b', 'wk_w', 'wk_b', 'wv_w', 'wv_b', 'wo_w', 'wo_b', 'wqi_w', 'wqi_b', 'wki_w', 'wki_b')}
    del _L0_attn_all

    def _L0_xattn_setup():
        import jax, jax.numpy as jnp
        import numpy as np
        EMBED_DIM = 256
        NUM_HEADS = 16
        HEAD_DIM = EMBED_DIM // NUM_HEADS
        SCALE_BASE = 128
        SEG_LENS = (256, 512, 1024)
        DIL_RATIOS = (1, 2, 4)
        NEG_INF = -100000000.0

        def _xpos(x, downscale):
            L, D = (x.shape[1], x.shape[2])
            half = D // 2
            scale_vec = (jnp.arange(0, D, 2, dtype=jnp.float32) + 0.4 * D) / (1.4 * D)
            min_pos = -L // 2
            power = jnp.arange(min_pos, L + min_pos, dtype=jnp.float32) / SCALE_BASE
            scale = scale_vec[None, :] ** power[:, None]
            inv_freq = 1.0 / 10000.0 ** (jnp.arange(half, dtype=jnp.float32) / half)
            sinusoid = jnp.arange(L, dtype=jnp.float32)[:, None] * inv_freq[None, :]
            sin, cos = (jnp.sin(sinusoid), jnp.cos(sinusoid))
            if downscale:
                scale = 1.0 / scale
            sin2 = jnp.repeat(sin * scale, 2, axis=-1)
            cos2 = jnp.repeat(cos * scale, 2, axis=-1)
            x1, x2 = (x[:, :, ::2], x[:, :, 1::2])
            rot = jnp.stack([-x2, x1], axis=-1).reshape(x.shape)
            return x * cos2 + rot * sin2

        def _dense_to_sparse(x, r):
            B, g, H, d = x.shape
            l, h2 = (g // r, H // r)
            x = x.reshape(B, l, r, r, h2, d)
            idx = jnp.arange(r)
            x = x[:, :, idx, idx]
            return x.reshape(B, l, H, d)

        def _sparse_to_dense(out, lse, r):
            B, l, H, d = out.shape
            h2 = H // r
            out = out.reshape(B, l, r, h2, d)
            eye = jnp.eye(r, dtype=out.dtype)
            o = jnp.einsum('blrhd,rs->bshlrd', out, eye).reshape(B, H, l * r, d)
            lse_t = lse.reshape(B, r, h2, l).transpose(0, 3, 2, 1)
            lse_d = jnp.where(jnp.eye(r, dtype=bool), lse_t[..., :, None], 0.0)
            lse_d = jnp.where(lse_d == 0, NEG_INF, lse_d)
            lse_d = lse_d.transpose(0, 4, 2, 1, 3).reshape(B, H, l * r, 1)
            return (o, lse_d)

        def _dilated_attention(query, key, value):
            b, L, E = query.shape
            H, d = (NUM_HEADS, E // NUM_HEADS)
            scaling = d ** (-0.5)

            def split_heads(x):
                return x.reshape(b, L, H, d).transpose(0, 2, 1, 3).reshape(b * H, L, d)
            q = _xpos(split_heads(query), downscale=False)
            k = _xpos(split_heads(key), downscale=True)
            v = split_heads(value)

            def to_blhd(x):
                return x.reshape(b, H, L, d).transpose(0, 2, 1, 3)
            q, k, v = (to_blhd(q), to_blhd(k), to_blhd(v))
            outs, lses = ([], [])
            for sl, r in zip(SEG_LENS, DIL_RATIOS):
                sl_ = min(sl, L)
                n = L // sl_

                def gather(x):
                    return _dense_to_sparse(x.reshape(b * n, sl_, H, d), r)
                qi, ki, vi = (gather(q), gather(k), gather(v))
                ls = qi.shape[1]
                scores = jnp.einsum('blhd,bshd->bhls', qi, ki) * scaling
                causal = jnp.tril(jnp.ones((ls, ls), dtype=bool))
                scores = jnp.where(causal, scores, -1000000000.0)
                lse = jax.nn.logsumexp(scores, axis=-1)
                probs = jnp.exp(scores - lse[..., None])
                o = jnp.einsum('bhls,bshd->blhd', probs, vi)
                o, lse_d = _sparse_to_dense(o, lse, r)
                o = o.reshape(b, n, H, sl_, d).transpose(0, 2, 1, 3, 4).reshape(b * H, L, d)
                lse_d = lse_d.reshape(b, n, H, sl_, 1).transpose(0, 2, 1, 3, 4).reshape(b * H, L, 1)
                outs.append(o)
                lses.append(lse_d)
            all_lse = jnp.stack(lses, axis=0)
            w = jnp.exp(all_lse - all_lse.max(axis=0, keepdims=True))
            w = w / w.sum(axis=0, keepdims=True)
            w = jax.lax.stop_gradient(w)
            attn = (jnp.stack(outs, axis=0) * w).sum(axis=0)
            return attn.reshape(b, H, L, d).transpose(0, 2, 1, 3).reshape(b, L, E)
        key = jax.random.key(seed)
        kq, kk, kv = jax.random.split(key, 3)
        shape = (1, 1024, EMBED_DIM)
        return {'query': jax.random.normal(kq, shape, dtype=jnp.float32), 'key': jax.random.normal(kk, shape, dtype=jnp.float32), 'value': jax.random.normal(kv, shape, dtype=jnp.float32)}
    _L0_xattn_all = _L0_xattn_setup()
    _L0_xattn_in = {k: v for k, v in _L0_xattn_all.items() if k in ()}
    del _L0_xattn_all

    def _L0_ffn_setup():
        import jax, jax.numpy as jnp
        import numpy as np
        TOP_K = 2
        key = jax.random.key(seed)
        k1, k2, k3, k4 = jax.random.split(key, 4)
        B_, S, D = (4, 2048, 256)
        E, R = (8, 16)
        x = jax.random.normal(k1, (B_, S, D), dtype=jnp.float32)
        Wg = jax.random.normal(k2, (D, E), dtype=jnp.float32) * 0.02
        A = jax.random.normal(k3, (E, D, R), dtype=jnp.float32) * 0.02
        Bm = jax.random.normal(k4, (E, R, D), dtype=jnp.float32) * 0.02
        return {'x': x, 'Wg': Wg, 'A': A, 'B': Bm}
    _L0_ffn_all = _L0_ffn_setup()
    _L0_ffn_in = {k: v for k, v in _L0_ffn_all.items() if k in ('Wg', 'A', 'B')}
    del _L0_ffn_all
    return {'x': x, 'ctx_1024': ctx_1024, 'L0_attn_wq_w': _L0_attn_in['wq_w'], 'L0_attn_wq_b': _L0_attn_in['wq_b'], 'L0_attn_wk_w': _L0_attn_in['wk_w'], 'L0_attn_wk_b': _L0_attn_in['wk_b'], 'L0_attn_wv_w': _L0_attn_in['wv_w'], 'L0_attn_wv_b': _L0_attn_in['wv_b'], 'L0_attn_wo_w': _L0_attn_in['wo_w'], 'L0_attn_wo_b': _L0_attn_in['wo_b'], 'L0_attn_wqi_w': _L0_attn_in['wqi_w'], 'L0_attn_wqi_b': _L0_attn_in['wqi_b'], 'L0_attn_wki_w': _L0_attn_in['wki_w'], 'L0_attn_wki_b': _L0_attn_in['wki_b'], 'L0_ffn_Wg': _L0_ffn_in['Wg'], 'L0_ffn_A': _L0_ffn_in['A'], 'L0_ffn_B': _L0_ffn_in['B']}

def reference(x, ctx_1024, L0_attn_wq_w, L0_attn_wq_b, L0_attn_wk_w, L0_attn_wk_b, L0_attn_wv_w, L0_attn_wv_b, L0_attn_wo_w, L0_attn_wo_b, L0_attn_wqi_w, L0_attn_wqi_b, L0_attn_wki_w, L0_attn_wki_b, L0_ffn_Wg, L0_ffn_A, L0_ffn_B):
    import jax
    import jax.numpy as jnp

    def _L0_attn_ref(x, wq_w, wq_b, wk_w, wk_b, wv_w, wv_b, wo_w, wo_b, wqi_w, wqi_b, wki_w, wki_b):
        import jax, jax.numpy as jnp
        import numpy as np
        import math
        D_MODEL = 256
        N_HEADS = 16
        D_HEAD = D_MODEL // N_HEADS
        TOP_K = 64
        WM = 128
        IDX_DIM = 64
        B, S = (2, 512)
        b, s, _ = x.shape
        scale = 1.0 / math.sqrt(D_HEAD)

        def heads(t):
            return t.reshape(b, s, N_HEADS, D_HEAD).transpose(0, 2, 1, 3)
        q = heads(x @ wq_w + wq_b)
        k = heads(x @ wk_w + wk_b)
        v = heads(x @ wv_w + wv_b)
        assoc_len = s - WM
        k_work, v_work = (k[:, :, -WM:], v[:, :, -WM:])
        k_assoc, v_assoc = (k[:, :, :assoc_len], v[:, :, :assoc_len])
        q_idx = x @ wqi_w + wqi_b
        k_idx = x[:, :assoc_len] @ wki_w + wki_b
        idx_scores = jax.nn.relu(jnp.einsum('bsi,bai->bsa', q_idx, k_idx))
        kk = min(TOP_K, assoc_len)
        _, top_idx = jax.lax.top_k(idx_scores, kk)
        gather = jax.vmap(lambda kv_b, i_b: kv_b[:, i_b])
        k_g = gather(k_assoc, top_idx)
        v_g = gather(v_assoc, top_idx)
        scores_assoc = jnp.einsum('bhsd,bhskd->bhsk', q, k_g) * scale
        scores_work = jnp.einsum('bhsd,bhwd->bhsw', q, k_work) * scale
        weights = jax.nn.softmax(jnp.concatenate([scores_assoc, scores_work], axis=-1), axis=-1)
        w_a, w_w = (weights[..., :kk], weights[..., kk:])
        out = jnp.einsum('bhsk,bhskd->bhsd', w_a, v_g) + jnp.einsum('bhsw,bhwd->bhsd', w_w, v_work)
        out = out.transpose(0, 2, 1, 3).reshape(b, s, D_MODEL)
        return out @ wo_w + wo_b

    def _L0_xattn_ref(query, key, value):
        import jax, jax.numpy as jnp
        import numpy as np
        EMBED_DIM = 256
        NUM_HEADS = 16
        HEAD_DIM = EMBED_DIM // NUM_HEADS
        SCALE_BASE = 128
        SEG_LENS = (256, 512, 1024)
        DIL_RATIOS = (1, 2, 4)
        NEG_INF = -100000000.0

        def _xpos(x, downscale):
            L, D = (x.shape[1], x.shape[2])
            half = D // 2
            scale_vec = (jnp.arange(0, D, 2, dtype=jnp.float32) + 0.4 * D) / (1.4 * D)
            min_pos = -L // 2
            power = jnp.arange(min_pos, L + min_pos, dtype=jnp.float32) / SCALE_BASE
            scale = scale_vec[None, :] ** power[:, None]
            inv_freq = 1.0 / 10000.0 ** (jnp.arange(half, dtype=jnp.float32) / half)
            sinusoid = jnp.arange(L, dtype=jnp.float32)[:, None] * inv_freq[None, :]
            sin, cos = (jnp.sin(sinusoid), jnp.cos(sinusoid))
            if downscale:
                scale = 1.0 / scale
            sin2 = jnp.repeat(sin * scale, 2, axis=-1)
            cos2 = jnp.repeat(cos * scale, 2, axis=-1)
            x1, x2 = (x[:, :, ::2], x[:, :, 1::2])
            rot = jnp.stack([-x2, x1], axis=-1).reshape(x.shape)
            return x * cos2 + rot * sin2

        def _dense_to_sparse(x, r):
            B, g, H, d = x.shape
            l, h2 = (g // r, H // r)
            x = x.reshape(B, l, r, r, h2, d)
            idx = jnp.arange(r)
            x = x[:, :, idx, idx]
            return x.reshape(B, l, H, d)

        def _sparse_to_dense(out, lse, r):
            B, l, H, d = out.shape
            h2 = H // r
            out = out.reshape(B, l, r, h2, d)
            eye = jnp.eye(r, dtype=out.dtype)
            o = jnp.einsum('blrhd,rs->bshlrd', out, eye).reshape(B, H, l * r, d)
            lse_t = lse.reshape(B, r, h2, l).transpose(0, 3, 2, 1)
            lse_d = jnp.where(jnp.eye(r, dtype=bool), lse_t[..., :, None], 0.0)
            lse_d = jnp.where(lse_d == 0, NEG_INF, lse_d)
            lse_d = lse_d.transpose(0, 4, 2, 1, 3).reshape(B, H, l * r, 1)
            return (o, lse_d)

        def _dilated_attention(query, key, value):
            b, L, E = query.shape
            H, d = (NUM_HEADS, E // NUM_HEADS)
            scaling = d ** (-0.5)

            def split_heads(x):
                return x.reshape(b, L, H, d).transpose(0, 2, 1, 3).reshape(b * H, L, d)
            q = _xpos(split_heads(query), downscale=False)
            k = _xpos(split_heads(key), downscale=True)
            v = split_heads(value)

            def to_blhd(x):
                return x.reshape(b, H, L, d).transpose(0, 2, 1, 3)
            q, k, v = (to_blhd(q), to_blhd(k), to_blhd(v))
            outs, lses = ([], [])
            for sl, r in zip(SEG_LENS, DIL_RATIOS):
                sl_ = min(sl, L)
                n = L // sl_

                def gather(x):
                    return _dense_to_sparse(x.reshape(b * n, sl_, H, d), r)
                qi, ki, vi = (gather(q), gather(k), gather(v))
                ls = qi.shape[1]
                scores = jnp.einsum('blhd,bshd->bhls', qi, ki) * scaling
                causal = jnp.tril(jnp.ones((ls, ls), dtype=bool))
                scores = jnp.where(causal, scores, -1000000000.0)
                lse = jax.nn.logsumexp(scores, axis=-1)
                probs = jnp.exp(scores - lse[..., None])
                o = jnp.einsum('bhls,bshd->blhd', probs, vi)
                o, lse_d = _sparse_to_dense(o, lse, r)
                o = o.reshape(b, n, H, sl_, d).transpose(0, 2, 1, 3, 4).reshape(b * H, L, d)
                lse_d = lse_d.reshape(b, n, H, sl_, 1).transpose(0, 2, 1, 3, 4).reshape(b * H, L, 1)
                outs.append(o)
                lses.append(lse_d)
            all_lse = jnp.stack(lses, axis=0)
            w = jnp.exp(all_lse - all_lse.max(axis=0, keepdims=True))
            w = w / w.sum(axis=0, keepdims=True)
            w = jax.lax.stop_gradient(w)
            attn = (jnp.stack(outs, axis=0) * w).sum(axis=0)
            return attn.reshape(b, H, L, d).transpose(0, 2, 1, 3).reshape(b, L, E)
        return _dilated_attention(query, key, value)

    def _L0_ffn_ref(x, Wg, A, B):
        import jax, jax.numpy as jnp
        import numpy as np
        TOP_K = 2
        D = x.shape[-1]
        E = Wg.shape[-1]
        xs = x.reshape(-1, D)
        gate_logits = xs @ Wg
        topw, sel = jax.lax.top_k(gate_logits, TOP_K)
        topw = jax.nn.softmax(topw.astype(jnp.float32), axis=-1).astype(x.dtype)
        cw = jnp.sum(jax.nn.one_hot(sel, E, dtype=x.dtype) * topw[..., None], axis=1)
        h = jnp.einsum('td,edr->ter', xs, A)
        hw = h * cw[..., None]
        out = jnp.einsum('ter,erd->td', hw, B)
        return out.reshape(x.shape)
    x = x + _L0_attn_ref(_layernorm(x, axis=-1), L0_attn_wq_w, L0_attn_wq_b, L0_attn_wk_w, L0_attn_wk_b, L0_attn_wv_w, L0_attn_wv_b, L0_attn_wo_w, L0_attn_wo_b, L0_attn_wqi_w, L0_attn_wqi_b, L0_attn_wki_w, L0_attn_wki_b)
    x = x + _L0_xattn_ref(_layernorm(x, axis=-1), ctx_1024, ctx_1024)
    x = x + _L0_ffn_ref(_layernorm(x, axis=-1), L0_ffn_Wg, L0_ffn_A, L0_ffn_B)
    return x

_drawn_inputs = setup_inputs


def setup_inputs(seed=0):
    import zlib

    import numpy as np

    out = dict(_drawn_inputs(seed))
    spreads = {'L0_attn_wq_b': (0.0, 0.8),
     'L0_attn_wk_b': (0.0, 0.8),
     'L0_attn_wv_b': (0.0, 0.1),
     'L0_attn_wo_b': (0.0, 0.1),
     'L0_attn_wqi_b': (0.0, 0.8),
     'L0_attn_wki_b': (0.0, 0.8)}
    factors = {'L0_attn_wq_w': 8.0,
     'L0_attn_wk_w': 8.0,
     'L0_attn_wv_w': 8.0,
     'L0_attn_wqi_w': 8.0,
     'L0_attn_wki_w': 8.0,
     'L0_ffn_Wg': 4.463,
     'L0_ffn_A': 3.808,
     'L0_ffn_B': 3.817}
    for name, (base, spread) in spreads.items():
        noise = np.random.default_rng([zlib.crc32(name.encode()), seed]).standard_normal(out[name].shape)
        drawn = base * np.exp(spread * noise) if base else spread * noise
        out[name] = jnp.asarray(drawn.astype(out[name].dtype))
    for name, factor in factors.items():
        out[name] = (out[name] * factor).astype(out[name].dtype)
    return out
```

```python
from contextlib import ExitStack

import concourse.bass as bass
from concourse import mybir

F32 = mybir.dt.float32
BF16 = mybir.dt.bfloat16
U32 = mybir.dt.uint32
ALU = mybir.AluOpType
ACT = mybir.ActivationFunctionType
AX = mybir.AxisListType

BATCH, SEQ, DIM = 16, 256, 256
HEADS, DH = 16, 16
IDX, TOPK, ASSOC = 64, 64, 128
EXPERTS, RANK = 8, 16
P = 128
TT = SEQ // P
HALVES = DIM // P
UNITS = HEADS // 2
GROUPS = HEADS // 4
PARTS = 3
PROD = 6 * DH
MROW = PROD
CROW = PROD + PARTS
ROWS = {1: CROW, 2: CROW + 4 * PARTS}
WIDTH = {1: 512, 2: 384}
NEG = -1.0e30
EPS = 1e-5
SCALE = DH ** -0.5
Q_RUNS = ((0, 3, 0), (3, 2, 0), (5, 1, 0))
K_RUNS = ((0, 1, 0), (1, 1, 0), (2, 1, 0), (3, 1, 1), (4, 1, 1), (5, 1, 2))
RUNS = {"q1": Q_RUNS, "q2": Q_RUNS, "k1": K_RUNS, "k2": K_RUNS}


def schedule():
    A = [[] for _ in range(UNITS)]
    B = [[] for _ in range(UNITS)]
    A[0] += [("load_x", 1), ("values", 2, 3, -4), ("misc_carry", None), ("m_turn", 1, 1, -1), ("split_low", "q2", -2)]
    A[1] += [("m_load", 1, 1, -1), ("o_turn", 2, 0, -4), ("stack_write", "q2", -2)]
    A[2] += [("values", 1, 0, -1), ("o_turn", 2, 1, -4), ("stack_read", "q2", -2)]
    A[3] += [("ln_stats", 3, -4), ("x_bias", 0)]
    A[4] += [("values", 1, 1, -1), ("ln_apply", 3, -4), ("rotate_k", -2)]
    A[5] += [("m_turn", 2, 0, -3), ("xn_turn", 3, -4), ("ln_stats", 1, 1)]
    A[6] += [("values", 1, 2, -1), ("m_load", 2, 0, -3), ("ln_apply", 1, 1)]
    A[7] += [("experts_in", -4), ("xn_turn", 1, 1), ("hold", -3)]
    B[0] += [("values", 1, 3, -1), ("m_turn", 2, 1, -3), ("mask_turn", 0), ("gate", -4)]
    B[1] += [("m_load", 2, 1, -3), ("o_turn", 1, 0, -1), ("project", "q1", 1)]
    B[2] += [("values", 2, 0, -3), ("o_turn", 1, 1, -1), ("split_low", "q1", 1), ("project", "k1", 1)]
    B[3] += [("stack_write", "q1", 1), ("o_features", -1), ("split_low", "k1", 1), ("k2_turn", -2)]
    B[4] += [("values", 2, 1, -3), ("stack_read", "q1", 1), ("out_proj", -1), ("stack_write", "k1", 1),
             ("project_v", 1), ("split_low", "k2", -2)]
    B[5] += [("ln_stats", 2, -1), ("m_turn", 1, 0, 0), ("stack_read", "k1", 1), ("stack_write", "k2", -2),
             ("h_turn", -4), ("ln_apply", 2, -1)]
    B[6] += [("values", 2, 2, -3), ("m_load", 1, 0, 0), ("idx_project", 1), ("rotate_q", -1),
             ("stack_read", "k2", -2), ("load_ctx", -1)]
    B[7] += [("idx_scores", 1), ("q2_turn", -1), ("experts_out", -4)]
    steps = []
    for u in range(UNITS):
        steps += [("scores", 1, u, -1), ("maxima", 2, u, -3), ("topk", u, 0)] + A[u]
    for u in range(UNITS):
        steps += [("scores", 2, u, -3), ("maxima", 1, u, 0)] + B[u]
    return steps


SCHEDULE = schedule()
LAGS = [s[-1] for s in SCHEDULE if s[-1] is not None]
FIRST = -max(LAGS)
LAST = BATCH - 1 - min(LAGS)
LOOP = 1 - min(LAGS)
TRIPS = (BATCH - max(LAGS) - LOOP) // 2


def decoder_layer(nc, x, ctx_in_dram, wq, wk, wv, wo, wi, bqk, bv, bo, bi, wgh, wb, rope_q, rope_k,
                  count_q, count_k, out):
    with ExitStack() as stack:
        def sb(name, shape, dt=F32):
            return stack.enter_context(nc.sbuf_tensor(name, shape, dt))

        def ps(name, shape, dt=F32):
            return stack.enter_context(nc.psum_tensor(name, shape, dt))

        def sem(name):
            return stack.enter_context(nc.semaphore(name))

        wq_sb, wk_sb, wv_sb, wo_sb = (sb(n, [P, HALVES, DIM]) for n in ("wq_sb", "wk_sb", "wv_sb", "wo_sb"))
        wi_sb = sb("wi_sb", [P, HALVES, 2 * IDX])
        wgh_sb = sb("wgh_sb", [P, HALVES, EXPERTS * RANK + EXPERTS])
        wb_sb = sb("wb_sb", [P, DIM])
        bqk_sb = sb("bqk_sb", [P, 4])
        bi_sb = sb("bi_sb", [IDX, 2])
        bv_sb, bo_sb = sb("bv_sb", [P, DIM]), sb("bo_sb", [P, DIM])
        rq_sb, rk_sb = sb("rq_sb", [P, 2, TT, DIM]), sb("rk_sb", [P, 2, TT, DIM])
        ident, ident_b = sb("ident", [P, P]), sb("ident_b", [P, P], BF16)
        causal_kq, causal_qk = sb("causal_kq", [P, 2, P], BF16), sb("causal_qk", [P, 2, P], BF16)
        eps_t, mhalf, one_t = (sb(n, [P, TT]) for n in ("eps_t", "mhalf", "one_t"))
        held_back = sb("held_back", [P, 1])
        eid = sb("eid", [P, EXPERTS])
        stk = {t: [sb(f"{t}_stack{i}", [P, HEADS, SEQ], BF16) for i in range(2)] for t in RUNS}
        parts = {t: sb(f"{t}_parts", [P, HALVES, PARTS, SEQ], BF16) for t in RUNS}
        rest = {t: sb(f"{t}_rest", [P, HALVES, SEQ]) for t in RUNS}
        vals = {a: [sb(f"vals{a}_{i}", [P, TT, HEADS, 32]) for i in range(2)] for a in (1, 2)}
        x_in = [sb(f"x_in{i}", [P, TT, DIM]) for i in range(2)]
        xb = [sb(f"xb{i}", [P, TT, DIM]) for i in range(2)]
        x1 = [sb(f"x1_{i}", [P, TT, DIM]) for i in range(2)]
        x1_held = [sb(f"x1_held{i}", [P, TT, DIM]) for i in range(2)]
        x2, y = sb("x2", [P, TT, DIM]), sb("y", [P, TT, DIM])
        xn = {i: sb(f"xn{i}", [P, TT, DIM]) for i in (1, 2, 3)}
        xnT = {i: sb(f"xnT{i}", [P, HALVES, SEQ]) for i in (1, 3)}
        ctx_t = sb("ctx_t", [P, TT, DIM])
        rot_a, rot_b = {}, {}
        for t in ("q2", "k2"):
            rot_a[t], rot_b[t] = sb(f"rot_a_{t}", [P, TT, DIM]), sb(f"rot_b_{t}", [P, TT, DIM])
        rotated = {t: sb(f"rotated_{t}", [P, TT, DIM]) for t in ("q2", "k2")}
        stats = {i: sb(f"stats{i}", [P, TT, 6]) for i in (1, 2, 3)}
        mv = {i: sb(f"mv{i}", [P, TT, 2]) for i in (1, 2, 3)}
        var_eps = {i: sb(f"var_eps{i}", [P, TT]) for i in (1, 2, 3)}
        rstd = {i: sb(f"rstd{i}", [P, TT]) for i in (1, 2, 3)}
        idxT = sb("idxT", [IDX, SEQ + ASSOC])
        work, max8 = sb("work", [P, TT, ASSOC]), sb("max8", [P, TT, 8])
        mask, maskT = sb("mask", [P, TT, ASSOC], BF16), sb("maskT", [P, SEQ], BF16)
        neg_max = {a: sb(f"neg_max{a}", [P, TT, HEADS]) for a in (1, 2)}
        m_rest = {a: sb(f"m_rest{a}", [P, TT, 8]) for a in (1, 2)}
        m_parts = {a: [sb(f"m_parts{a}_{g}", [P, TT, PARTS * 8], BF16) for g in range(2)] for a in (1, 2)}
        m_rows = {a: [sb(f"m_rows{a}_{g}", [PARTS * 8, SEQ], BF16) for g in range(2)] for a in (1, 2)}
        expo = [sb(f"expo{i}", [P, 2, 512]) for i in range(4)]
        oT = {a: sb(f"oT{a}", [P, GROUPS, SEQ]) for a in (1, 2)}
        rsum = {a: sb(f"rsum{a}", [P, TT, HEADS]) for a in (1, 2)}
        o = {a: sb(f"o{a}", [P, TT, DIM]) for a in (1, 2)}
        o1T = sb("o1T", [P, HALVES, SEQ])
        logits, top8 = sb("logits", [P, TT, EXPERTS]), sb("top8", [P, TT, 8])
        top_i, top_f = sb("top_i", [P, TT, 8], U32), sb("top_f", [P, TT, 2])
        gap, gexp, gden = sb("gap", [P, TT]), sb("gexp", [P, TT]), sb("gden", [P, TT])
        w_top = sb("w_top", [P, 2, TT])
        gw = sb("gw", [P, 2, TT, EXPERTS])
        cw = sb("cw", [P, TT, EXPERTS])
        hid = sb("hid", [P, TT, EXPERTS * RANK])
        hidw, hT = sb("hidw", [P, TT, EXPERTS * RANK]), sb("hT", [P, SEQ])

        st = [ps(f"st{i}", [P, 2, 512]) for i in range(2)]
        mx = ps("mx", [P, 2, 512])
        pv = ps("pv", [P, 2, SEQ])
        misc = ps("misc", [P, 512])

        scr = {t: nc.dram_tensor(f"scr_{t}", [HALVES, PARTS, P, SEQ], BF16).ap() for t in RUNS}
        m_scr = {a: [nc.dram_tensor(f"m_scr{a}_{g}", [PARTS * 8, SEQ], BF16).ap() for g in range(2)] for a in (1, 2)}

        loaded = sem("loaded")
        zeroed, consts = sem("zeroed"), sem("consts")
        x_loaded, ctx_loaded = sem("x_loaded"), sem("ctx_loaded")
        sp_ready = sem("sp_ready")
        xb_done = sem("xb_done")
        ln_bn = sem("ln_bn")
        ln_mv = {i: sem(f"ln_mv{i}") for i in (1, 2, 3)}
        ln_rstd = {i: sem(f"ln_rstd{i}") for i in (1, 2, 3)}
        ln_done = {i: sem(f"ln_done{i}") for i in (1, 2, 3)}
        turned = {i: sem(f"turned{i}") for i in (1, 3)}
        turned_out = {i: sem(f"turned_out{i}") for i in (1, 3)}
        raw_ready = {t: sem(f"raw_{t}") for t in RUNS}
        high_done = {t: sem(f"high_{t}") for t in RUNS}
        rest_done = {t: sem(f"rest_{t}") for t in RUNS}
        low_done = {t: sem(f"low_{t}") for t in RUNS}
        scr_done = {t: sem(f"scr_done_{t}") for t in RUNS}
        stk_done = {t: sem(f"stk_done_{t}") for t in RUNS}
        v_raw, v_done = sem("v_raw"), {a: sem(f"v_done{a}") for a in (1, 2)}
        ip_raw, ip_done = sem("ip_raw"), sem("ip_done")
        is_raw, is_done = sem("is_raw"), sem("is_done")
        topk_step = sem("topk_step")
        mask_done, maskT_raw, maskT_done = sem("mask_done"), sem("maskT_raw"), sem("maskT_done")
        mx_ready = {a: sem(f"mx_ready{a}") for a in (1, 2)}
        mx_done = {a: sem(f"mx_done{a}") for a in (1, 2)}
        m_step = {a: sem(f"m_step{a}") for a in (1, 2)}
        m_raw = {a: sem(f"m_raw{a}") for a in (1, 2)}
        m_out = {a: sem(f"m_out{a}") for a in (1, 2)}
        m_written = {a: [sem(f"m_written{a}_{g}") for g in range(2)] for a in (1, 2)}
        m_done = {a: [sem(f"m_done{a}_{g}") for g in range(2)] for a in (1, 2)}
        st_ready = {a: sem(f"st_ready{a}") for a in (1, 2)}
        exp_done = {a: sem(f"exp_done{a}") for a in (1, 2)}
        pv_ready = {a: sem(f"pv_ready{a}") for a in (1, 2)}
        pv_done = {a: sem(f"pv_done{a}") for a in (1, 2)}
        o_raw = {a: sem(f"o_raw{a}") for a in (1, 2)}
        o_rcp = {a: sem(f"o_rcp{a}") for a in (1, 2)}
        o_done = {a: sem(f"o_done{a}") for a in (1, 2)}
        of_raw, of_done = sem("of_raw"), sem("of_done")
        wo_raw, x1_done = sem("wo_raw"), sem("x1_done")
        held = sem("held")
        x2_done = sem("x2_done")
        ra_done = {t: sem(f"ra_done_{t}") for t in ("q2", "k2")}
        rb_done = {t: sem(f"rb_done_{t}") for t in ("q2", "k2")}
        rot_done = {t: sem(f"rot_done_{t}") for t in ("q2", "k2")}
        gh_raw, gh_done = sem("gh_raw"), sem("gh_done")
        g_max = sem("g_max")
        g_step, g_exp = sem("g_step"), sem("g_exp")
        ht_raw, ht_done = sem("ht_raw"), sem("ht_done")
        fo_raw, y_done, stored = sem("fo_raw"), sem("y_done"), sem("stored")
        G_STEPS = 9

        def count(per, b, k):
            return min(b * per + k, BATCH * per) if isinstance(b, int) else b * per + k

        def some(per, b, k):
            return not isinstance(b, int) or b * per + k > 0

        def iterate(eng, handlers):
            def iteration(n, parity):
                for name, *args, lag in SCHEDULE:
                    if name not in handlers:
                        continue
                    if lag is None:
                        handlers[name](n)
                        continue
                    b = n + lag
                    if not (isinstance(b, int) and not 0 <= b < BATCH):
                        handlers[name](b, (parity + lag) % 2, *args)

            for n in range(FIRST, LOOP):
                iteration(n, n % 2)
            with eng.Fori(LOOP, LOOP + 2 * TRIPS - 1, 2) as n:
                iteration(n, LOOP % 2)
                iteration(n + 1, (LOOP + 1) % 2)
            for n in range(LOOP + 2 * TRIPS, LAST + 1):
                iteration(n, n % 2)

        tok = "(t p) d -> p t d"
        LOADS = [(wq_sb, wq.rearrange("(f p) n -> p f n", p=P)), (wk_sb, wk.rearrange("(f p) n -> p f n", p=P)),
                 (wv_sb, wv.rearrange("(f p) n -> p f n", p=P)), (wo_sb, wo.rearrange("(f p) n -> p f n", p=P)),
                 (wi_sb, wi.rearrange("(f p) n -> p f n", p=P)), (wgh_sb, wgh.rearrange("(f p) n -> p f n", p=P)),
                 (wb_sb, wb), (rq_sb, rope_q.rearrange("c (t p) d -> p c t d", p=P)),
                 (rk_sb, rope_k.rearrange("c (t p) d -> p c t d", p=P)),
                 (bqk_sb, bqk), (bi_sb, bi)]
        LOADS += [(bv_sb, bv.partition_broadcast(P)), (bo_sb, bo.partition_broadcast(P))]
        for i in range(2):
            LOADS += [(stk["q2"][i][CROW:ROWS[2]], count_q), (stk["k2"][i][MROW:ROWS[2]], count_k),
                      (stk["k1"][i][MROW:CROW], count_k[0:PARTS])]

        block = stack.enter_context(nc.Block())

        @block.sync
        def _(sp):
            for n, (dst, src) in enumerate(LOADS):
                sp.dma_start(dst if isinstance(dst, bass.AP) else dst[:], src).then_inc(loaded, 16)

            def load_x(b, par):
                if some(1, b - 2, 1):
                    sp.wait_ge(xb_done, count(1, b - 2, 1))
                sp.sem_inc(sp_ready, 1)
                if some(1, b - 1, 1):
                    sp.wait_ge(ln_done[1], count(1, b - 1, 1))
                sp.sem_inc(sp_ready, 1)
                sp.dma_start(x_in[par][:], x[b].rearrange(tok, p=P)).then_inc(x_loaded, 16)

            def load_ctx(b, par):
                if some(1, b - 1, 1):
                    sp.wait_ge(rot_done["k2"], count(1, b - 1, 1))
                if some(1, b - 1, 1):
                    sp.wait_ge(v_done[2], count(1, b - 1, 1))
                sp.sem_inc(sp_ready, 1)
                sp.dma_start(ctx_t[:], ctx_in_dram[b].rearrange(tok, p=P)).then_inc(ctx_loaded, 16)

            def stack_write(b, par, t):
                if some(16 * len(RUNS[t]), b, 0):
                    sp.wait_ge(stk_done[t], count(16 * len(RUNS[t]), b, 0))
                sp.wait_ge(low_done[t], count(2, b, 2))
                for f in range(HALVES):
                    sp.dma_start(scr[t][f].rearrange("r p s -> p r s"), parts[t][:, f]).then_inc(scr_done[t], 16)

            def stack_read(b, par, t):
                a = int(t[1])
                if some(UNITS, b - 1, 0):
                    sp.wait_ge(st_ready[a], count(UNITS, b - 1, 0))
                sp.wait_ge(scr_done[t], count(16 * HALVES, b, 16 * HALVES))
                rows = scr[t].rearrange("f r (d g) s -> f (r d) (g s)", d=DH)
                for blk, n, part in RUNS[t]:
                    dst = stk[t][par][blk * DH:(blk + n) * DH].rearrange("p (f g) s -> p f (g s)", f=HALVES)
                    sp.dma_start(dst, rows[:, part * DH:(part + n) * DH].rearrange("f r s -> r f s"))\
                      .then_inc(stk_done[t], 16)

            def m_turn(b, par, a, g):
                sp.wait_ge(m_out[a], count(2, b, g + 1))
                sp.dma_start(m_scr[a][g], m_rows[a][g][:]).then_inc(m_written[a][g], 16)

            def m_load(b, par, a, g):
                sp.wait_ge(m_written[a][g], count(16, b, 16))
                sp.dma_start(stk[f"q{a}"][par][MROW:MROW + PARTS, 8 * g:8 * g + 8, :],
                             m_scr[a][g].rearrange("(r h) s -> r h s", r=PARTS)).then_inc(m_done[a][g], 16)

            def hold(b, par):
                if some(2, b - 1, 0):
                    sp.wait_ge(x2_done, count(2, b - 1, 0))
                sp.wait_ge(x1_done, count(1, b, 1))
                sp.dma_start(x1_held[par][:], x1[par][:]).then_inc(held, 16)

            def experts_out(b, par):
                sp.wait_ge(y_done, count(1, b, 1))
                sp.sem_inc(sp_ready, 1)
                sp.dma_start(out[b].rearrange(tok, p=P), y[:]).then_inc(stored, 16)

            iterate(sp, dict(load_x=load_x, load_ctx=load_ctx, stack_write=stack_write, stack_read=stack_read,
                             m_turn=m_turn, m_load=m_load, hold=hold, experts_out=experts_out))
            sp.wait_ge(stored, 16 * BATCH)
            for t in RUNS:
                sp.wait_ge(scr_done[t], 16 * HALVES * BATCH)
            for a in (1, 2):
                for g in range(2):
                    sp.wait_ge(m_written[a][g], 16 * BATCH)

        @block.gpsimd
        def _(pool):
            for a in (1, 2):
                for v in vals[a]:
                    pool.memset(v[:], 1.0)
            pool.memset(eps_t[:], EPS)
            pool.memset(mhalf[:], -0.5)
            pool.memset(one_t[:], 1.0)
            for t in (ident, ident_b, causal_kq, causal_qk):
                pool.memset(t[:], 0.0).then_inc(zeroed, 1)
            for e in range(EXPERTS):
                pool.memset(eid[:, e:e + 1], float(e))
            pool.wait_ge(zeroed, 4)
            for t in (ident, ident_b):
                pool.affine_select(out=t[:], in_=t[:], compare_op=ALU.not_equal, fill=1.0, base=0,
                                   pattern=[[-1, P]], channel_multiplier=1)
            pool.affine_select(out=causal_kq[:], in_=causal_kq[:], compare_op=ALU.is_ge, fill=NEG, base=0,
                               pattern=[[0, 2], [1, P]], channel_multiplier=-1)
            pool.affine_select(out=causal_qk[:], in_=causal_qk[:], compare_op=ALU.is_ge, fill=NEG, base=0,
                               pattern=[[0, 2], [-1, P]], channel_multiplier=1).then_inc(consts, 1)
            pool.wait_ge(loaded, 16 * len(LOADS))

            def ln_stats(b, par, i):
                if some(1, b, 0):
                    pool.wait_ge(ln_done[i], count(1, b, 0))
                pool.wait_ge(ln_mv[i], count(1, b, 1))
                pool.tensor_tensor(var_eps[i][:], mv[i][:, :, 1], eps_t[:], ALU.add).then_inc(ln_rstd[i], 1)
                pool.wait_ge(ln_rstd[i], count(2, b, 1))
                pool.tensor_tensor(rstd[i][:], var_eps[i][:], mhalf[:], ALU.pow).then_inc(ln_rstd[i], 1)

            def x_bias(b, par):
                if some(1, b - 2, 1):
                    pool.wait_ge(x1_done, count(1, b - 2, 1))
                pool.wait_ge(x_loaded, count(16, b, 16))
                pool.tensor_tensor(xb[par][:], x_in[par][:], bo_sb[:].unsqueeze(1).broadcast_to([P, TT, DIM]),
                                   ALU.add).then_inc(xb_done, 1)

            def split_low(b, par, t):
                if some(16 * HALVES, b, 0):
                    pool.wait_ge(scr_done[t], count(16 * HALVES, b, 0))
                pool.wait_ge(rest_done[t], count(1, b, 1))
                pool.tensor_tensor(parts[t][:, :, 1, :], rest[t][:],
                                   one_t[:].unsqueeze(2).broadcast_to([P, HALVES, SEQ]), ALU.mult).then_inc(low_done[t], 1)
                pool.wait_ge(low_done[t], count(2, b, 1))
                pool.tensor_tensor(parts[t][:, :, 2, :], rest[t][:], parts[t][:, :, 1, :], ALU.subtract)\
                    .then_inc(low_done[t], 1)

            def swapped(t, src, table):
                s = src[:].rearrange("p t (i e) -> p t i e", e=2)
                d = rot_b[t][:].rearrange("p t (i e) -> p t i e", e=2)
                w = table[:, 1].rearrange("p t (i e) -> p t i e", e=2)
                pool.tensor_tensor(d[:, :, :, 0], s[:, :, :, 1], w[:, :, :, 0], ALU.mult)
                pool.tensor_tensor(d[:, :, :, 1], s[:, :, :, 0], w[:, :, :, 1], ALU.mult).then_inc(rb_done[t], 1)

            def rotation_sum(t):
                lie = "p t (f g d) -> p (t f) g d"
                pool.tensor_tensor(rotated[t][:].rearrange("p t (f d g) -> p (t f) g d", f=HALVES, d=DH),
                                   rot_a[t][:].rearrange(lie, f=HALVES, d=DH),
                                   rot_b[t][:].rearrange(lie, f=HALVES, d=DH), ALU.add).then_inc(rot_done[t], 1)

            def rotate_k(b, par):
                pool.wait_ge(ctx_loaded, count(16, b, 16))
                pool.tensor_tensor(rot_a["k2"][:], ctx_t[:], rk_sb[:, 0], ALU.mult).then_inc(ra_done["k2"], 1)
                swapped("k2", ctx_t, rk_sb)
                if some(1, b, 0):
                    pool.wait_ge(raw_ready["k2"], count(1, b, 0))
                pool.wait_ge(ra_done["k2"], count(1, b, 1))
                pool.wait_ge(rb_done["k2"], count(1, b, 1))
                rotation_sum("k2")

            def rotate_q(b, par):
                pool.wait_ge(ln_done[2], count(1, b, 1))
                swapped("q2", xn[2], rq_sb)
                if some(1, b, 0):
                    pool.wait_ge(raw_ready["q2"], count(1, b, 0))
                pool.wait_ge(ra_done["q2"], count(1, b, 1))
                pool.wait_ge(rb_done["q2"], count(1, b, 1))
                rotation_sum("q2")

            iterate(pool, dict(ln_stats=ln_stats, x_bias=x_bias, split_low=split_low, rotate_k=rotate_k,
                               rotate_q=rotate_q))

        @block.scalar
        def _(act):
            act.wait_ge(loaded, 16 * len(LOADS))
            act.wait_ge(consts, 1)

            def scores(b, par, a, u):
                if some(GROUPS, b, u // 2 - 1):
                    act.wait_ge(pv_ready[a], count(GROUPS, b, u // 2 - 1))
                if u < 4:
                    if some(GROUPS, b - 2 if a == 1 else b + 3, 0):
                        act.wait_ge(pv_ready[3 - a], count(GROUPS, b - 2 if a == 1 else b + 3, 0))
                act.wait_ge(st_ready[a], count(UNITS, b, u + 1))
                act.activation(expo[u % 4][:, :, 0:WIDTH[a]], st[u % 2][:, :, 0:WIDTH[a]], ACT.Exp, scale=SCALE)\
                   .then_inc(exp_done[a], 1)

            def values(b, par, a, g):
                act.wait_ge(pv_ready[a], count(GROUPS, b, g + 1))
                act.activation(oT[a][:, g, :], pv[:, g % 2, :], ACT.Copy).then_inc(pv_done[a], 1)

            def m_turn(b, par, a, g):
                if some(16, b, 0):
                    act.wait_ge(m_written[a][g], count(16, b, 0))
                act.wait_ge(m_raw[a], count(2, b, g + 1))
                act.activation(m_rows[a][g][:], misc[0:PARTS * 8, 0:P].bitcast(BF16), ACT.Copy).then_inc(m_out[a], 1)

            def xn_turn(b, par, i):
                act.wait_ge(turned[i], count(1, b, 1))
                act.activation(xnT[i][:].rearrange("p f s -> p (f s)"), misc[:], ACT.Copy).then_inc(turned_out[i], 1)

            def high(b, t):
                if some(16 * HALVES, b, 0):
                    act.wait_ge(scr_done[t], count(16 * HALVES, b, 0))
                act.wait_ge(raw_ready[t], count(1, b, 1))
                for f in range(HALVES):
                    src = misc[:, f * SEQ:(f + 1) * SEQ]
                    if t[1] == "1":
                        c = f + (2 if t == "k1" else 0)
                        i = act.activation(parts[t][:, f, 0, :], src, ACT.Identity, bias=bqk_sb[:, c:c + 1])
                    else:
                        i = act.activation(parts[t][:, f, 0, :], src, ACT.Copy)
                i.then_inc(high_done[t], 1)

            def idx_project(b, par):
                act.wait_ge(ip_raw, count(1, b, 1))
                act.activation(idxT[:, 0:SEQ], misc[0:IDX, 0:SEQ], ACT.Identity, bias=bi_sb[:, 0:1])
                act.activation(idxT[:, SEQ:SEQ + ASSOC], misc[0:IDX, SEQ:SEQ + ASSOC], ACT.Identity,
                               bias=bi_sb[:, 1:2]).then_inc(ip_done, 1)

            def idx_scores(b, par):
                if some(1, b, 0):
                    act.wait_ge(mask_done, count(1, b, 0))
                act.wait_ge(is_raw, count(1, b, 1))
                act.activation(work[:].rearrange("p t k -> p (t k)"), misc[:, 0:TT * ASSOC], ACT.Relu)\
                   .then_inc(is_done, 1)

            def mask_turn(b, par):
                act.wait_ge(maskT_raw, count(1, b, 1))
                act.activation(maskT[:], misc[:, 0:P].bitcast(BF16), ACT.Copy).then_inc(maskT_done, 1)

            def o_features(b, par):
                act.wait_ge(of_raw, count(1, b, 1))
                act.activation(o1T[:].rearrange("p f s -> p (f s)"), misc[:], ACT.Copy).then_inc(of_done, 1)

            def rotate_k(b, par):
                if some(GROUPS, b - 1, 0):
                    act.wait_ge(pv_ready[2], count(GROUPS, b - 1, 0))
                act.wait_ge(ctx_loaded, count(16, b, 16))
                for t in range(TT):
                    i = act.activation(vals[2][par][:, t, :, 0:DH], ctx_t[:, t, :].rearrange("p (h d) -> p h d", d=DH),
                                       ACT.Copy)
                i.then_inc(v_done[2], 1)

            def gate(b, par):
                act.wait_ge(g_step, count(G_STEPS, b, 2))
                act.activation(gexp[:], gap[:], ACT.Exp).then_inc(g_exp, 1)

            def experts_in(b, par):
                if some(G_STEPS, b, 0):
                    act.wait_ge(g_step, count(G_STEPS, b, 0))
                act.wait_ge(gh_raw, count(1, b, 1))
                src = misc[:, 0:TT * 136].rearrange("p (t c) -> p t c", t=TT)
                act.activation(hid[:], src[:, :, 0:P], ACT.Copy)
                act.activation(logits[:], src[:, :, P:P + EXPERTS], ACT.Copy).then_inc(gh_done, 1)

            def h_turn(b, par):
                act.wait_ge(ht_raw, count(1, b, 1))
                act.activation(hT[:], misc[:, 0:SEQ], ACT.Copy).then_inc(ht_done, 1)

            iterate(act, dict(scores=scores, values=values, m_turn=m_turn, xn_turn=xn_turn,
                              project=lambda b, par, t: high(b, t), k2_turn=lambda b, par: high(b, "k2"),
                              q2_turn=lambda b, par: high(b, "q2"), idx_project=idx_project, idx_scores=idx_scores,
                              mask_turn=mask_turn, o_features=o_features, rotate_k=rotate_k, gate=gate,
                              experts_in=experts_in, h_turn=h_turn))

        @block.vector
        def _(dve):
            dve.wait_ge(loaded, 16 * len(LOADS))
            dve.wait_ge(consts, 1)
            LN_IN = {1: lambda par: x_in[par], 2: lambda par: x1[par], 3: lambda par: x2}

            def maxima(b, par, a, u):
                dve.wait_ge(mx_ready[a], count(UNITS, b, u + 1))
                if a == 1:
                    src = mx[:].rearrange("p j (t k) -> p t j k", t=TT)
                    i = dve.tensor_reduce(neg_max[a][:, :, 2 * u:2 * u + 2], src, AX.X, ALU.max, negate=True)
                else:
                    dve.tensor_reduce(neg_max[a][:, 0, 2 * u:2 * u + 2], mx[:, :, 0:P], AX.X, ALU.max, negate=True)
                    i = dve.tensor_reduce(neg_max[a][:, 1, 2 * u:2 * u + 2], mx[:, :, P:3 * P], AX.X, ALU.max,
                                          negate=True)
                i.then_inc(mx_done[a], 1)

            def m_turn(b, par, a, g):
                src, dst = neg_max[a][:, :, 8 * g:8 * g + 8], m_parts[a][g]
                if some(2, b - 1, g + 1):
                    dve.wait_ge(m_raw[a], count(2, b - 1, g + 1))
                dve.wait_ge(mx_done[a], count(UNITS, b, 4 * g + 4))
                dve.tensor_copy(dst[:, :, 0:8], src).then_inc(m_step[a], 1)
                dve.wait_ge(m_step[a], count(8, b, 4 * g + 1))
                dve.tensor_tensor(m_rest[a][:], src, dst[:, :, 0:8], ALU.subtract).then_inc(m_step[a], 1)
                dve.wait_ge(m_step[a], count(8, b, 4 * g + 2))
                dve.tensor_copy(dst[:, :, 8:16], m_rest[a][:]).then_inc(m_step[a], 1)
                dve.wait_ge(m_step[a], count(8, b, 4 * g + 3))
                dve.tensor_tensor(dst[:, :, 16:24], m_rest[a][:], dst[:, :, 8:16], ALU.subtract)\
                   .then_inc(m_step[a], 1)

            def topk(b, par, r):
                if r == 0:
                    dve.wait_ge(is_done, count(1, b, 1))
                    dve.memset(held_back[:], 0.0)
                for t in range(TT):
                    if r > 0:
                        dve.wait_ge(topk_step, 4 * r - 1 + t)
                    dve.max(max8[:, t, :], work[:, t, :]).then_inc(topk_step, 1)
                for t in range(TT):
                    dve.wait_ge(topk_step, 4 * r + 1 + t)
                    dve.match_replace(work[:, t, :], max8[:, t, :], work[:, t, :], -1.0).then_inc(topk_step, 1)
                if r == 7:
                    dve.wait_ge(topk_step, 32)
                    dve.sem_clear(topk_step)
                    if some(UNITS, b, 0):
                        dve.wait_ge(mx_ready[1], count(UNITS, b, 0))
                    if some(1, b, 0):
                        dve.wait_ge(maskT_raw, count(1, b, 0))
                    dve.tensor_scalar(mask[:], work[:], 0.0, NEG, ALU.is_ge, ALU.mult).then_inc(mask_done, 1)

            def ln_stats(b, par, i):
                src = LN_IN[i](par)
                if i == 1:
                    dve.wait_ge(x_loaded, count(16, b, 16))
                if i == 2:
                    dve.wait_ge(x1_done, count(1, b, 1))
                if i == 3:
                    dve.wait_ge(x2_done, count(2, b, 2))
                if some(2, b, 0):
                    dve.wait_ge(ln_rstd[i], count(2, b, 0))
                for t in range(TT):
                    ins = dve.bn_stats(stats[i][:, t, :], src[:, t, :])
                ins.then_inc(ln_bn, 1)
                dve.wait_ge(ln_bn, 1)
                dve.sem_clear(ln_bn)
                for t in range(TT):
                    ins = dve.bn_aggr(mv[i][:, t, :], stats[i][:, t, :])
                ins.then_inc(ln_mv[i], 1)

            def ln_apply(b, par, i):
                src = LN_IN[i](par)
                if i in turned:
                    if some(1, b, 0):
                        dve.wait_ge(turned[i], count(1, b, 0))
                else:
                    if some(1, b, 0):
                        dve.wait_ge(rot_done["q2"], count(1, b, 0))
                dve.wait_ge(ln_mv[i], count(1, b, 1))
                dve.wait_ge(ln_rstd[i], count(2, b, 2))
                for t in range(TT):
                    ins = dve.tensor_scalar(xn[i][:, t, :], src[:, t, :], mv[i][:, t, 0:1], rstd[i][:, t:t + 1],
                                            ALU.subtract, ALU.mult)
                ins.then_inc(ln_done[i], 1)

            def rotate_q(b, par):
                dve.wait_ge(ln_done[2], count(1, b, 1))
                dve.tensor_tensor(rot_a["q2"][:], xn[2][:], rq_sb[:, 0], ALU.mult).then_inc(ra_done["q2"], 1)

            def split_rest(b, t):
                if some(2, b, 0):
                    dve.wait_ge(low_done[t], count(2, b, 0))
                dve.wait_ge(raw_ready[t], count(1, b, 1))
                dve.wait_ge(high_done[t], count(1, b, 1))
                if t[1] == "1":
                    for f in range(HALVES):
                        c = f + (2 if t == "k1" else 0)
                        i = dve.scalar_tensor_tensor(out=rest[t][:, f, :], in0=misc[:, f * SEQ:(f + 1) * SEQ],
                                                     scalar=bqk_sb[:, c:c + 1], in1=parts[t][:, f, 0, :],
                                                     op0=ALU.add, op1=ALU.subtract)
                else:
                    i = dve.tensor_tensor(rest[t][:], misc[:].rearrange("p (f s) -> p f s", f=HALVES),
                                          parts[t][:, :, 0, :], ALU.subtract)
                i.then_inc(rest_done[t], 1)

            def project_v(b, par):
                if some(GROUPS, b - 1, 0):
                    dve.wait_ge(pv_ready[1], count(GROUPS, b - 1, 0))
                dve.wait_ge(v_raw, count(1, b, 1))
                for t in range(TT):
                    i = dve.tensor_tensor(vals[1][par][:, t, :, 0:DH],
                                          misc[:, t * DIM:(t + 1) * DIM].rearrange("p (h d) -> p h d", d=DH),
                                          bv_sb[:].rearrange("p (h d) -> p h d", d=DH), ALU.add)
                i.then_inc(v_done[1], 1)

            def o_turn(b, par, a, t):
                src = misc[:].rearrange("p (h c) -> p h c", c=32)
                dve.wait_ge(o_raw[a], count(2, b, t + 1))
                dve.reciprocal(rsum[a][:, t, :], src[:, :, DH]).then_inc(o_rcp[a], 1)
                dve.wait_ge(o_rcp[a], count(2, b, t + 1))
                dst = o[a][:, t, :].rearrange("p (h d) -> p h d", d=DH)
                dve.tensor_tensor(dst, src[:, :, 0:DH], rsum[a][:, t, :].unsqueeze(2).broadcast_to([P, HEADS, DH]),
                                  ALU.mult).then_inc(o_done[a], 1)
                if a == 2:
                    dve.wait_ge(held, count(16, b, 16))
                    dve.wait_ge(o_done[a], count(2, b, t + 1))
                    dve.tensor_tensor(x2[:, t, :], x1_held[par][:, t, :], o[a][:, t, :], ALU.add).then_inc(x2_done, 1)

            def out_proj(b, par):
                if some(16, b - 1, 0):
                    dve.wait_ge(held, count(16, b - 1, 0))
                dve.wait_ge(xb_done, count(1, b, 1))
                dve.wait_ge(wo_raw, count(1, b, 1))
                dve.tensor_tensor(x1[par][:], misc[:].rearrange("p (t d) -> p t d", t=TT), xb[par][:], ALU.add)\
                   .then_inc(x1_done, 1)

            def gate(b, par):
                dve.wait_ge(gh_done, count(1, b, 1))
                dve.memset(held_back[:], 0.0)
                for t in range(TT):
                    i = dve.max(top8[:, t, :], logits[:, t, :])
                i.then_inc(g_max, 1)
                dve.wait_ge(g_max, 1)
                dve.sem_clear(g_max)
                for t in range(TT):
                    i = dve.max_index(top_i[:, t, :], top8[:, t, :], logits[:, t, :])
                i.then_inc(g_step, 1)
                dve.tensor_tensor(gap[:], top8[:, :, 1], top8[:, :, 0], ALU.subtract).then_inc(g_step, 1)
                dve.wait_ge(g_step, count(G_STEPS, b, 1))
                dve.tensor_copy(top_f[:], top_i[:, :, 0:2]).then_inc(g_step, 1)
                dve.wait_ge(g_exp, count(1, b, 1))
                dve.tensor_scalar(gden[:], gexp[:], 1.0, None, ALU.add).then_inc(g_step, 1)
                dve.wait_ge(g_step, count(G_STEPS, b, 4))
                dve.reciprocal(w_top[:, 0, :], gden[:]).then_inc(g_step, 1)
                dve.wait_ge(g_step, count(G_STEPS, b, 5))
                dve.tensor_tensor(w_top[:, 1, :], gexp[:], w_top[:, 0, :], ALU.mult).then_inc(g_step, 1)
                dve.wait_ge(g_step, count(G_STEPS, b, 6))
                for k in range(2):
                    for t in range(TT):
                        i = dve.tensor_scalar(gw[:, k, t, :], eid[:], top_f[:, t, k:k + 1], w_top[:, k, t:t + 1],
                                              ALU.is_equal, ALU.mult)
                i.then_inc(g_step, 1)
                dve.wait_ge(g_step, count(G_STEPS, b, 7))
                dve.tensor_tensor(cw[:], gw[:, 0], gw[:, 1], ALU.add).then_inc(g_step, 1)
                if some(1, b, 0):
                    dve.wait_ge(ht_raw, count(1, b, 0))
                dve.wait_ge(g_step, count(G_STEPS, b, 8))
                for t in range(TT):
                    i = dve.tensor_tensor(hidw[:, t, :].rearrange("p (e r) -> p e r", e=EXPERTS),
                                          hid[:, t, :].rearrange("p (e r) -> p e r", e=EXPERTS),
                                          cw[:, t, :].unsqueeze(2).broadcast_to([P, EXPERTS, RANK]), ALU.mult)
                i.then_inc(g_step, 1)

            def experts_out(b, par):
                if some(16, b, 0):
                    dve.wait_ge(stored, count(16, b, 0))
                dve.wait_ge(fo_raw, count(1, b, 1))
                dve.tensor_tensor(y[:], misc[:].rearrange("p (t d) -> p t d", t=TT), x2[:], ALU.add)\
                   .then_inc(y_done, 1)

            iterate(dve, dict(maxima=maxima, m_turn=m_turn, topk=topk, ln_stats=ln_stats, ln_apply=ln_apply,
                              rotate_q=rotate_q, project=lambda b, par, t: split_rest(b, t),
                              k2_turn=lambda b, par: split_rest(b, "k2"), q2_turn=lambda b, par: split_rest(b, "q2"),
                              project_v=project_v, o_turn=o_turn, out_proj=out_proj, gate=gate,
                              experts_out=experts_out))

        @block.tensor
        def _(pe):
            pe.wait_ge(loaded, 16 * len(LOADS))
            pe.wait_ge(consts, 1)
            misc_b = misc[:, 0:P].bitcast(BF16)
            taken = [None]

            def misc_carry(n):
                taken[0] = None
                if some(1, n, 1):
                    pe.wait_ge(is_done, count(1, n, 1))
                if some(1, n - 2, 1):
                    pe.wait_ge(rest_done["q2"], count(1, n - 2, 1))
                if some(1, n - 5, 1):
                    pe.wait_ge(y_done, count(1, n - 5, 1))

            def two_diagonals(tile, j):
                return tile[:, j, :].rearrange("p (t c) -> p t c", t=2)[:, :, 0:P]

            def scores(b, par, a, u):
                if u == 0:
                    if a == 1:
                        pe.wait_ge(maskT_done, count(1, b, 1))
                if u % 4 == 0:
                    pe.wait_ge(m_done[a][u // 4], count(16, b, 16))
                if some(UNITS, b, u - 1):
                    pe.wait_ge(exp_done[a], count(UNITS, b, u - 1))
                if u < 2:
                    if some(UNITS, b - 2 if a == 1 else b + 3, 0):
                        pe.wait_ge(exp_done[3 - a], count(UNITS, b - 2 if a == 1 else b + 3, 0))
                q, k, rows, dst = stk[f"q{a}"][par], stk[f"k{a}"][par], ROWS[a], st[u % 2]
                for j in range(2):
                    h = 2 * u + j
                    pe.matmul(dst[:, j, 0:SEQ], k[0:rows, h, 0:P], q[0:rows, h, :], start=True, stop=False)
                    if a == 1:
                        pe.matmul(dst[:, j, 0:SEQ], ident_b[:], maskT[:], start=False, stop=True)
                        i = pe.matmul(dst[:, j, SEQ:2 * SEQ], k[0:rows, h, P:SEQ], q[0:rows, h, :],
                                      start=True, stop=True)
                    else:
                        pe.matmul(dst[:, j, SEQ:SEQ + P], k[0:rows, h, P:SEQ], q[0:rows, h, P:SEQ],
                                  start=False, stop=False)
                        i = pe.matmul(two_diagonals(dst, j), ident_b[:], causal_kq[:], start=False, stop=True)
                i.then_inc(st_ready[a], 1)

            def maxima(b, par, a, u):
                if u == 0:
                    for t in (f"q{a}", f"k{a}"):
                        pe.wait_ge(stk_done[t], count(16 * len(RUNS[t]), b, 16 * len(RUNS[t])))
                    if a == 1:
                        pe.wait_ge(mask_done, count(1, b, 1))
                    if some(UNITS, b - 2 if a == 1 else b + 3, 0):
                        pe.wait_ge(mx_done[3 - a], count(UNITS, b - 2 if a == 1 else b + 3, 0))
                if some(UNITS, b, u):
                    pe.wait_ge(mx_done[a], count(UNITS, b, u))
                q, k = stk[f"q{a}"][par], stk[f"k{a}"][par]
                for j in range(2):
                    h = 2 * u + j
                    if a == 1:
                        for t in range(TT):
                            pe.matmul(mx[:, j, t * SEQ:(t + 1) * SEQ], q[0:PROD, h, t * P:(t + 1) * P],
                                      k[0:PROD, h, :], start=(t == 0), stop=False)
                        i = pe.matmul(two_diagonals(mx, j), ident_b[:], mask[:], start=False, stop=True)
                    else:
                        pe.matmul(mx[:, j, 0:P], q[0:PROD, h, 0:P], k[0:PROD, h, 0:P], start=True, stop=False)
                        pe.matmul(mx[:, j, P:3 * P], q[0:PROD, h, P:SEQ], k[0:PROD, h, :], start=False, stop=False)
                        i = pe.matmul(two_diagonals(mx, j), ident_b[:], causal_qk[:], start=False, stop=True)
                i.then_inc(mx_ready[a], 1)

            def values(b, par, a, g):
                if g == 0:
                    pe.wait_ge(v_done[a], count(1, b, 1))
                pe.wait_ge(exp_done[a], count(UNITS, b, 2 * g + 2))
                if some(GROUPS, b, g - 1):
                    pe.wait_ge(pv_done[a], count(GROUPS, b, g - 1))
                if g < 2:
                    if some(GROUPS, b - 2 if a == 1 else b + 3, 0):
                        pe.wait_ge(pv_done[3 - a], count(GROUPS, b - 2 if a == 1 else b + 3, 0))
                for kt in range(TT):
                    for c in range(4):
                        h, src = 4 * g + c, expo[(2 * g + c // 2) % 4]
                        q0 = P * kt if a == 2 else 0
                        i = pe.matmul(pv[32 * c:32 * c + 32, g % 2, q0:SEQ], vals[a][par][:, kt, h, :],
                                      src[:, c % 2, kt * SEQ:kt * SEQ + SEQ - q0], start=(kt == 0), stop=(kt == 1))
                i.then_inc(pv_ready[a], 1)

            def m_turn(b, par, a, g):
                if taken[0]:
                    pe.wait_ge(*taken[0])
                pe.wait_ge(m_step[a], count(8, b, 4 * g + 4))
                for t in range(TT):
                    i = pe.transpose(misc_b[0:PARTS * 8, t * P:(t + 1) * P], m_parts[a][g][:, t, :], ident_b[:])
                i.then_inc(m_raw[a], 1)
                taken[0] = (m_out[a], count(2, b, g + 1))

            def turn(src):
                for f in range(HALVES):
                    for t in range(TT):
                        i = pe.transpose(misc[:, f * SEQ + t * P:f * SEQ + (t + 1) * P],
                                         src[:, t, f * P:(f + 1) * P], ident[:])
                return i

            def xn_turn(b, par, i):
                if taken[0]:
                    pe.wait_ge(*taken[0])
                pe.wait_ge(ln_done[i], count(1, b, 1))
                turn(xn[i]).then_inc(turned[i], 1)
                taken[0] = (turned_out[i], count(1, b, 1))

            def project(b, par, t):
                w = wq_sb if t == "q1" else wk_sb
                if taken[0]:
                    pe.wait_ge(*taken[0])
                pe.wait_ge(turned_out[1], count(1, b, 1))
                for f in range(HALVES):
                    for c in range(HALVES):
                        i = pe.matmul(misc[:, f * SEQ:(f + 1) * SEQ], w[:, c, f * P:(f + 1) * P], xnT[1][:, c, :],
                                      start=(c == 0), stop=(c == 1))
                i.then_inc(raw_ready[t], 1)
                taken[0] = (rest_done[t], count(1, b, 1))

            def project_v(b, par):
                if taken[0]:
                    pe.wait_ge(*taken[0])
                for t in range(TT):
                    for c in range(HALVES):
                        i = pe.matmul(misc[:, t * DIM:(t + 1) * DIM], xnT[1][:, c, t * P:(t + 1) * P], wv_sb[:, c, :],
                                      start=(c == 0), stop=(c == 1))
                i.then_inc(v_raw, 1)
                taken[0] = (v_done[1], count(1, b, 1))

            def idx_project(b, par):
                if taken[0]:
                    pe.wait_ge(*taken[0])
                for k, n in ((0, SEQ), (1, ASSOC)):
                    for c in range(HALVES):
                        i = pe.matmul(misc[0:IDX, k * SEQ:k * SEQ + n], wi_sb[:, c, k * IDX:(k + 1) * IDX],
                                      xnT[1][:, c, 0:n], start=(c == 0), stop=(c == 1))
                i.then_inc(ip_raw, 1)
                taken[0] = (ip_done, count(1, b, 1))

            def idx_scores(b, par):
                if taken[0]:
                    pe.wait_ge(*taken[0])
                pe.wait_ge(ip_done, count(1, b, 1))
                for t in range(TT):
                    i = pe.matmul(misc[:, t * ASSOC:(t + 1) * ASSOC], idxT[:, t * P:(t + 1) * P],
                                  idxT[:, SEQ:SEQ + ASSOC], start=True, stop=True)
                i.then_inc(is_raw, 1)
                taken[0] = (is_done, count(1, b, 1))

            def mask_turn(b, par):
                if taken[0]:
                    pe.wait_ge(*taken[0])
                pe.wait_ge(mask_done, count(1, b, 1))
                for t in range(TT):
                    i = pe.transpose(misc_b[:, t * P:(t + 1) * P], mask[:, t, :], ident_b[:])
                i.then_inc(maskT_raw, 1)
                taken[0] = (maskT_done, count(1, b, 1))

            def o_turn(b, par, a, t):
                if taken[0]:
                    pe.wait_ge(*taken[0])
                pe.wait_ge(pv_done[a], count(GROUPS, b, GROUPS))
                for g in range(GROUPS):
                    i = pe.transpose(misc[:, g * P:(g + 1) * P], oT[a][:, g, t * P:(t + 1) * P], ident[:])
                i.then_inc(o_raw[a], 1)
                taken[0] = (o_done[a], count(2, b, t + 1))

            def o_features(b, par):
                if taken[0]:
                    pe.wait_ge(*taken[0])
                pe.wait_ge(o_done[1], count(2, b, 2))
                turn(o[1]).then_inc(of_raw, 1)
                taken[0] = (of_done, count(1, b, 1))

            def out_proj(b, par):
                if taken[0]:
                    pe.wait_ge(*taken[0])
                pe.wait_ge(of_done, count(1, b, 1))
                for t in range(TT):
                    for c in range(HALVES):
                        i = pe.matmul(misc[:, t * DIM:(t + 1) * DIM], o1T[:, c, t * P:(t + 1) * P], wo_sb[:, c, :],
                                      start=(c == 0), stop=(c == 1))
                i.then_inc(wo_raw, 1)
                taken[0] = (x1_done, count(1, b, 1))

            def rotated_turn(b, t):
                if taken[0]:
                    pe.wait_ge(*taken[0])
                pe.wait_ge(rot_done[t], count(1, b, 1))
                turn(rotated[t]).then_inc(raw_ready[t], 1)
                taken[0] = (rest_done[t], count(1, b, 1))

            def experts_in(b, par):
                if taken[0]:
                    pe.wait_ge(*taken[0])
                pe.wait_ge(turned_out[3], count(1, b, 1))
                for t in range(TT):
                    for c in range(HALVES):
                        i = pe.matmul(misc[:, t * 136:(t + 1) * 136], xnT[3][:, c, t * P:(t + 1) * P],
                                      wgh_sb[:, c, :], start=(c == 0), stop=(c == 1))
                i.then_inc(gh_raw, 1)
                taken[0] = (gh_done, count(1, b, 1))

            def h_turn(b, par):
                if taken[0]:
                    pe.wait_ge(*taken[0])
                pe.wait_ge(g_step, count(G_STEPS, b, G_STEPS))
                for t in range(TT):
                    i = pe.transpose(misc[:, t * P:(t + 1) * P], hidw[:, t, :], ident[:])
                i.then_inc(ht_raw, 1)
                taken[0] = (ht_done, count(1, b, 1))

            def experts_out(b, par):
                if taken[0]:
                    pe.wait_ge(*taken[0])
                pe.wait_ge(ht_done, count(1, b, 1))
                for t in range(TT):
                    i = pe.matmul(misc[:, t * DIM:(t + 1) * DIM], hT[:, t * P:(t + 1) * P], wb_sb[:],
                                  start=True, stop=True)
                i.then_inc(fo_raw, 1)
                taken[0] = (y_done, count(1, b, 1))

            handlers = dict(misc_carry=misc_carry, scores=scores, maxima=maxima, values=values, m_turn=m_turn, xn_turn=xn_turn,
                            project=project, project_v=project_v, idx_project=idx_project, idx_scores=idx_scores,
                            mask_turn=mask_turn, o_turn=o_turn, o_features=o_features, out_proj=out_proj,
                            k2_turn=lambda b, par: rotated_turn(b, "k2"), q2_turn=lambda b, par: rotated_turn(b, "q2"),
                            experts_in=experts_in, h_turn=h_turn, experts_out=experts_out)

            iterate(pe, handlers)


_CONSTS = ("rope_q", "rope_k", "count_q", "count_k")
_INS = ["x", "ctx", "wq", "wk", "wv", "wo", "wi", "bqk", "bv", "bo", "bi", "wgh", "wb", *_CONSTS]


def constants():
    import numpy as np

    f = np.float32
    half = DH // 2
    scale_vec = (np.arange(0, DH, 2, dtype=f) + f(0.4 * DH)) / f(1.4 * DH)
    power = np.arange(-SEQ // 2, SEQ - SEQ // 2, dtype=f) / f(128)
    scale = scale_vec[None, :] ** power[:, None]
    inv_freq = f(1.0) / f(10000.0) ** (np.arange(half, dtype=f) / f(half))
    angle = np.arange(SEQ, dtype=f)[:, None] * inv_freq[None, :]
    tables = []
    for s in (scale, f(1.0) / scale):
        cos, sin = np.cos(angle) * s, np.sin(angle) * s
        c = np.tile(np.repeat(cos, 2, axis=1), (1, HEADS))
        signed = np.tile(np.stack([-sin, sin], axis=-1).reshape(SEQ, DH), (1, HEADS))
        tables.append(np.stack([c, signed]).astype(f))
    b16 = np.dtype("bfloat16")
    count_q = np.zeros((4, PARTS, HEADS, SEQ), b16)
    h, q = np.arange(HEADS)[:, None], np.arange(SEQ)[None, :]
    for i in range(4):
        n = np.ones((HEADS, SEQ))
        for r in (2, 4):
            j = h // (HEADS // r)
            n = n + ((q % r == j) & (i % r == j))
        left = np.log(n) / SCALE
        for part in range(PARTS):
            count_q[i, part] = left.astype(b16)
            left = left - count_q[i, part].astype(np.float64)
    count_k = np.ones((PARTS + 4 * PARTS, HEADS, SEQ), b16)
    for i in range(4):
        count_k[PARTS + PARTS * i:PARTS + PARTS * (i + 1)] = (np.arange(SEQ) % 4 == i).astype(b16)
    return tables[0], tables[1], count_q.reshape(4 * PARTS, HEADS, SEQ), count_k


def kernel(**inputs):
    import numpy as np
    import concourse.bacc as bacc
    from concourse.bass_utils import run_bass_kernel_spmd

    g = {k: np.asarray(v) for k, v in inputs.items()}
    order = np.arange(DIM).reshape(HALVES, HEADS // HALVES, DH).transpose(0, 2, 1).reshape(-1)
    a, f = "L0_attn_", "L0_ffn_"
    arrays = dict(
        x=g["x"], ctx=g["ctx_1024"], wq=g[a + "wq_w"][:, order], wk=g[a + "wk_w"][:, order], wv=g[a + "wv_w"],
        wo=g[a + "wo_w"], wi=np.concatenate([g[a + "wqi_w"], g[a + "wki_w"]], axis=1), 
        bqk=np.concatenate([g[a + "wq_b"][order], g[a + "wk_b"][order]]).reshape(4, P).T, bv=g[a + "wv_b"], bo=g[a + "wo_b"],
        bi=np.stack([g[a + "wqi_b"], g[a + "wki_b"]], axis=1),
        wgh=np.concatenate([g[f + "A"].transpose(1, 0, 2).reshape(DIM, EXPERTS * RANK), g[f + "Wg"]], axis=1),
        wb=g[f + "B"].reshape(EXPERTS * RANK, DIM), **dict(zip(_CONSTS, constants())))
    arrays = {k: np.ascontiguousarray(v) for k, v in arrays.items()}
    nc = bacc.Bacc("TRN2", target_bir_lowering=False, num_devices=1)
    args = [nc.dram_tensor(f"in_{n}", arrays[n].shape, mybir.dt.from_np(arrays[n].dtype), kind="ExternalInput").ap()
            for n in _INS]
    args.append(nc.dram_tensor("out_0", (BATCH, SEQ, DIM), F32, kind="ExternalOutput").ap())
    decoder_layer(nc, *args)
    r = run_bass_kernel_spmd(nc, [{f"in_{n}": arrays[n] for n in _INS}], core_ids=[0])
    return r.results[0]["out_0"]
```

```python
from contextlib import ExitStack

import concourse.bass as bass
from concourse import mybir

F32 = mybir.dt.float32
BF16 = mybir.dt.bfloat16
U32 = mybir.dt.uint32
ALU = mybir.AluOpType
ACT = mybir.ActivationFunctionType
AX = mybir.AxisListType

BATCH, SEQ, DIM = 16, 256, 256
HEADS, DH = 16, 16
IDX, TOPK, ASSOC = 64, 64, 128
EXPERTS, RANK = 8, 16
P = 128
TT = SEQ // P
HALVES = DIM // P
UNITS = HEADS // 2
GROUPS = HEADS // 4
PARTS = 3
PROD = 6 * DH
MROW = PROD
CROW = PROD + PARTS
ROWS = {1: CROW, 2: CROW + 4 * PARTS}
WIDTH = {1: 512, 2: 384}
NEG = -1.0e30
EPS = 1e-5
SCALE = DH ** -0.5
Q_RUNS = ((0, 3, 0), (3, 2, 0), (5, 1, 0))
K_RUNS = ((0, 1, 0), (1, 1, 0), (2, 1, 0), (3, 1, 1), (4, 1, 1), (5, 1, 2))
RUNS = {"q1": Q_RUNS, "q2": Q_RUNS, "k1": K_RUNS, "k2": K_RUNS}


def schedule():
    A = [[[], [], []] for _ in range(UNITS)]
    B = [[[], [], []] for _ in range(UNITS)]
    A[0][0] += [("load_x", 1), ("misc_carry", None)]
    A[0][2] += [("topk", 4, 0), ("values", 2, 3, -4)]
    A[1][0] += [("m_turn", 1, 1, -1), ("stack_read", "k2", -2)]
    A[1][1] += [("o_turn", 2, 0, -4)]
    A[1][2] += [("ln_stats", 1, 1), ("ctx_values", -2)]
    A[2][0] += [("m_load", 1, 1, -1)]
    A[2][1] += [("o_turn", 2, 1, -4)]
    A[2][2] += [("ln_apply", 1, 1), ("values", 1, 0, -1), ("x_residual", -4)]
    A[3][0] += [("q2_turn", -2), ("load_ctx", -1)]
    A[3][2] += [("topk", 5, 0), ("m_split", 2, 0, -3), ("ln_stats", 3, -4), ("split_rest", "q2", -2),
                ("split_low", "q2", -2)]
    A[4][1] += [("xn_turn", 1, 1)]
    A[4][2] += [("topk", 6, 0), ("values", 1, 1, -1), ("ln_apply", 3, -4), ("x_bias", 0)]
    A[5][1] += [("m_turn", 2, 0, -3), ("stack_write", "q2", -2), ("project", "q1", 1)]
    A[5][2] += [("split_rest", "q1", 1), ("topk", 7, 0)]
    A[6][0] += [("m_load", 2, 0, -3), ("stack_read", "q2", -2)]
    A[6][1] += [("xn_turn", 3, -4)]
    A[6][2] += [("values", 1, 2, -1), ("split_low", "q1", 1)]
    A[7][0] += [("project", "k1", 1), ("split_rest", "k1", 1), ("hold", -3)]
    A[7][1] += [("experts_in", -4)]
    A[7][2] += [("m_split", 2, 1, -3), ("gate", -4)]
    B[0][0] += [("stack_write", "q1", 1)]
    B[0][1] += [("mask_turn", 0)]
    B[0][2] += [("values", 1, 3, -1), ("gate_weights", -4), ("split_low", "k1", 1)]
    B[1][0] += [("m_turn", 2, 1, -3)]
    B[1][1] += [("idx_project", 1)]
    B[1][2] += [("rotate_k", -1)]
    B[2][0] += [("m_load", 2, 1, -3), ("stack_read", "q1", 1), ("o_turn", 1, 0, -1)]
    B[2][1] += [("o_turn", 1, 1, -1)]
    B[2][2] += [("values", 2, 0, -3)]
    B[3][0] += [("stack_write", "k1", 1)]
    B[3][1] += [("idx_scores", 1), ("h_turn", -4)]
    B[3][2] += [("topk", 0, 1), ("m_split", 1, 0, 0)]
    B[4][0] += [("o_features", -1)]
    B[4][2] += [("topk", 1, 1), ("values", 2, 1, -3), ("split_rest", "k2", -1), ("split_low", "k2", -1)]
    B[5][0] += [("k2_turn", -1), ("out_proj", -1)]
    B[5][1] += [("m_turn", 1, 0, 0), ("stack_read", "k1", 1)]
    B[5][2] += [("ln_stats", 2, -1)]
    B[6][0] += [("topk", 2, 1), ("m_load", 1, 0, 0), ("experts_out", -4), ("stack_write", "k2", -1)]
    B[6][1] += [("project_v", 1)]
    B[6][2] += [("values", 2, 2, -3)]
    B[7][2] += [("topk", 3, 1), ("m_split", 1, 1, 0), ("ln_apply", 2, -1), ("rotate_q", -1)]
    steps = []
    for u in range(UNITS):
        steps += A[u][0] + [("scores", 1, u, -1)] + A[u][1] + [("maxima", 2, u, -3)] + A[u][2]
    for u in range(UNITS):
        steps += B[u][0] + [("scores", 2, u, -3)] + B[u][1] + [("maxima", 1, u, 0)] + B[u][2]
    return steps


SCHEDULE = schedule()
USES_MISC = ("m_turn", "xn_turn", "project", "project_v", "idx_project", "idx_scores", "mask_turn", "o_turn",
             "o_features", "out_proj", "k2_turn", "q2_turn", "experts_in", "h_turn", "experts_out")
BANK = {s[:-1]: i % 2 for i, s in enumerate(s for s in SCHEDULE if s[0] in USES_MISC)}
LAGS = [s[-1] for s in SCHEDULE if s[-1] is not None]
FIRST = -max(LAGS)
LAST = BATCH - 1 - min(LAGS)
LOOP = 1 - min(LAGS)
TRIPS = (BATCH - max(LAGS) - LOOP) // 2


def decoder_layer(nc, x, ctx_in_dram, wq, wk, wv, wo, wi, bqk, bv, bo, bi, wgh, wb, rope_q, rope_k,
                  count_q, count_k, out):
    with ExitStack() as stack:
        def sb(name, shape, dt=F32):
            return stack.enter_context(nc.sbuf_tensor(name, shape, dt))

        def ps(name, shape, dt=F32):
            return stack.enter_context(nc.psum_tensor(name, shape, dt))

        def sem(name):
            return stack.enter_context(nc.semaphore(name))

        wq_sb, wk_sb, wv_sb, wo_sb = (sb(n, [P, HALVES, DIM]) for n in ("wq_sb", "wk_sb", "wv_sb", "wo_sb"))
        wi_sb = sb("wi_sb", [P, HALVES, 2 * IDX])
        wgh_sb = sb("wgh_sb", [P, HALVES, EXPERTS * RANK + EXPERTS])
        wb_sb = sb("wb_sb", [P, DIM])
        bqk_sb = sb("bqk_sb", [P, 4])
        bi_sb = sb("bi_sb", [IDX, 2])
        bv_sb, bo_sb = sb("bv_sb", [P, DIM]), sb("bo_sb", [P, DIM])
        rq_sb, rk_sb = sb("rq_sb", [P, 2, TT, DIM]), sb("rk_sb", [P, 2, TT, DIM])
        ident, ident_b = sb("ident", [P, P]), sb("ident_b", [P, P], BF16)
        causal_kq, causal_qk = sb("causal_kq", [P, 2, P], BF16), sb("causal_qk", [P, 2, P], BF16)
        eps_t, mhalf, one_t = (sb(n, [P, TT]) for n in ("eps_t", "mhalf", "one_t"))
        held_back = sb("held_back", [P, 1])
        eid = sb("eid", [P, EXPERTS])
        stk = {t: [sb(f"{t}_stack{i}", [P, HEADS, SEQ], BF16) for i in range(2)] for t in RUNS}
        parts = {t: sb(f"{t}_parts", [P, HALVES, PARTS, SEQ], BF16) for t in RUNS}
        rest = {t: sb(f"{t}_rest", [P, HALVES, SEQ]) for t in RUNS}
        vals = {a: [sb(f"vals{a}_{i}", [P, TT, HEADS, 32]) for i in range(2)] for a in (1, 2)}
        x_in = [sb(f"x_in{i}", [P, TT, DIM]) for i in range(2)]
        xb = [sb(f"xb{i}", [P, TT, DIM]) for i in range(2)]
        x1 = [sb(f"x1_{i}", [P, TT, DIM]) for i in range(2)]
        x1_held = [sb(f"x1_held{i}", [P, TT, DIM]) for i in range(2)]
        x2, y = sb("x2", [P, TT, DIM]), sb("y", [P, TT, DIM])
        xn = {i: sb(f"xn{i}", [P, TT, DIM]) for i in (1, 2, 3)}
        xnT = {i: sb(f"xnT{i}", [P, HALVES, SEQ]) for i in (1, 3)}
        ctx_t = sb("ctx_t", [P, TT, DIM])
        rot_a, rot_b = {}, {}
        for t in ("q2", "k2"):
            rot_a[t], rot_b[t] = sb(f"rot_a_{t}", [P, TT, DIM]), sb(f"rot_b_{t}", [P, TT, DIM])
        rotated = {t: sb(f"rotated_{t}", [P, TT, DIM]) for t in ("q2", "k2")}
        stats = {i: sb(f"stats{i}", [P, TT, 6]) for i in (1, 2, 3)}
        mv = {i: sb(f"mv{i}", [P, TT, 2]) for i in (1, 2, 3)}
        var_eps = {i: sb(f"var_eps{i}", [P, TT]) for i in (1, 2, 3)}
        rstd = {i: sb(f"rstd{i}", [P, TT]) for i in (1, 2, 3)}
        idxT = sb("idxT", [IDX, SEQ + ASSOC])
        work, max8 = sb("work", [P, TT, ASSOC]), sb("max8", [P, TT, 8])
        mask, maskT = sb("mask", [P, TT, ASSOC], BF16), sb("maskT", [P, SEQ], BF16)
        neg_max = {a: sb(f"neg_max{a}", [P, TT, HEADS]) for a in (1, 2)}
        m_rest = {a: sb(f"m_rest{a}", [P, TT, 8]) for a in (1, 2)}
        m_parts = {a: [sb(f"m_parts{a}_{g}", [P, TT, PARTS * 8], BF16) for g in range(2)] for a in (1, 2)}
        m_rows = {a: [sb(f"m_rows{a}_{g}", [PARTS * 8, SEQ], BF16) for g in range(2)] for a in (1, 2)}
        expo = [sb(f"expo{i}", [P, 2, 512]) for i in range(4)]
        oT = {a: sb(f"oT{a}", [P, GROUPS, SEQ]) for a in (1, 2)}
        rsum = {a: sb(f"rsum{a}", [P, TT, HEADS]) for a in (1, 2)}
        o = {a: sb(f"o{a}", [P, TT, DIM]) for a in (1, 2)}
        o1T = sb("o1T", [P, HALVES, SEQ])
        logits, top8 = sb("logits", [P, TT, EXPERTS]), sb("top8", [P, TT, 8])
        top_i, top_f = sb("top_i", [P, TT, 8], U32), sb("top_f", [P, TT, 2])
        gap, gexp, gden = sb("gap", [P, TT]), sb("gexp", [P, TT]), sb("gden", [P, TT])
        w_top = sb("w_top", [P, 2, TT])
        gw = sb("gw", [P, 2, TT, EXPERTS])
        cw = sb("cw", [P, TT, EXPERTS])
        hid = sb("hid", [P, TT, EXPERTS * RANK])
        hidw, hT = sb("hidw", [P, TT, EXPERTS * RANK]), sb("hT", [P, SEQ])

        st = [ps(f"st{i}", [P, 512]) for i in range(3)]
        mx = [ps(f"mx{i}", [P, 512]) for i in range(2)]
        pv = ps("pv", [P, 2, SEQ])
        misc_banks = [ps(f"misc{i}", [P, 512]) for i in range(2)]

        scr = {t: nc.dram_tensor(f"scr_{t}", [HALVES, PARTS, P, SEQ], BF16).ap() for t in RUNS}
        m_scr = {a: [nc.dram_tensor(f"m_scr{a}_{g}", [PARTS * 8, SEQ], BF16).ap() for g in range(2)] for a in (1, 2)}

        loaded_early, loaded_late = sem("loaded_early"), sem("loaded_late")
        zeroed, consts = sem("zeroed"), sem("consts")
        x_loaded, ctx_loaded = sem("x_loaded"), sem("ctx_loaded")
        sp_ready = sem("sp_ready")
        xb_done = sem("xb_done")
        ln_bn = sem("ln_bn")
        ln_mv = {i: sem(f"ln_mv{i}") for i in (1, 2, 3)}
        ln_rstd = {i: sem(f"ln_rstd{i}") for i in (1, 2, 3)}
        ln_done = {i: sem(f"ln_done{i}") for i in (1, 2, 3)}
        turned = {i: sem(f"turned{i}") for i in (1, 3)}
        turned_out = {i: sem(f"turned_out{i}") for i in (1, 3)}
        raw_ready = {t: sem(f"raw_{t}") for t in RUNS}
        high_done = {t: sem(f"high_{t}") for t in RUNS}
        rest_done = {t: sem(f"rest_{t}") for t in RUNS}
        low_done = {t: sem(f"low_{t}") for t in RUNS}
        scr_done = {t: sem(f"scr_done_{t}") for t in RUNS}
        stk_done = {t: sem(f"stk_done_{t}") for t in RUNS}
        v_raw, v_done = sem("v_raw"), {a: sem(f"v_done{a}") for a in (1, 2)}
        ip_raw, ip_done = sem("ip_raw"), sem("ip_done")
        is_raw, is_done = sem("is_raw"), sem("is_done")
        topk_step = sem("topk_step")
        mask_done, maskT_raw, maskT_done = sem("mask_done"), sem("maskT_raw"), sem("maskT_done")
        mx_ready = {a: sem(f"mx_ready{a}") for a in (1, 2)}
        mx_done = {a: sem(f"mx_done{a}") for a in (1, 2)}
        m_step = {a: sem(f"m_step{a}") for a in (1, 2)}
        m_raw = {a: sem(f"m_raw{a}") for a in (1, 2)}
        m_out = {a: sem(f"m_out{a}") for a in (1, 2)}
        m_written = {a: [sem(f"m_written{a}_{g}") for g in range(2)] for a in (1, 2)}
        m_done = {a: [sem(f"m_done{a}_{g}") for g in range(2)] for a in (1, 2)}
        st_ready = {a: sem(f"st_ready{a}") for a in (1, 2)}
        exp_done = {a: sem(f"exp_done{a}") for a in (1, 2)}
        pv_ready = {a: sem(f"pv_ready{a}") for a in (1, 2)}
        pv_done = {a: sem(f"pv_done{a}") for a in (1, 2)}
        o_raw = {a: sem(f"o_raw{a}") for a in (1, 2)}
        o_rcp = {a: sem(f"o_rcp{a}") for a in (1, 2)}
        o_done = {a: sem(f"o_done{a}") for a in (1, 2)}
        of_raw, of_done = sem("of_raw"), sem("of_done")
        wo_raw, x1_done = sem("wo_raw"), sem("x1_done")
        held = sem("held")
        x2_done = sem("x2_done")
        ra_done = {t: sem(f"ra_done_{t}") for t in ("q2", "k2")}
        rb_done = {t: sem(f"rb_done_{t}") for t in ("q2", "k2")}
        rot_done = {t: sem(f"rot_done_{t}") for t in ("q2", "k2")}
        gh_raw, gh_done = sem("gh_raw"), sem("gh_done")
        g_max = sem("g_max")
        g_step, g_exp = sem("g_step"), sem("g_exp")
        ht_raw, ht_done = sem("ht_raw"), sem("ht_done")
        fo_raw, y_done, stored = sem("fo_raw"), sem("y_done"), sem("stored")
        G_STEPS = 9

        def count(per, b, k):
            return min(b * per + k, BATCH * per) if isinstance(b, int) else b * per + k

        def some(per, b, k):
            return not isinstance(b, int) or b * per + k > 0

        def first(b):
            return isinstance(b, int) and b == 0

        def iterate(eng, handlers):
            def iteration(n, parity):
                for name, *args, lag in SCHEDULE:
                    if name not in handlers:
                        continue
                    if lag is None:
                        handlers[name](n)
                        continue
                    b = n + lag
                    if not (isinstance(b, int) and not 0 <= b < BATCH):
                        handlers[name](b, (parity + lag) % 2, *args)

            for n in range(FIRST, LOOP):
                iteration(n, n % 2)
            with eng.Fori(LOOP, LOOP + 2 * TRIPS - 1, 2) as n:
                iteration(n, LOOP % 2)
                iteration(n + 1, (LOOP + 1) % 2)
            for n in range(LOOP + 2 * TRIPS, LAST + 1):
                iteration(n, n % 2)

        def misc_of(*step):
            return misc_banks[BANK[step]]

        def st_of(a, h):
            return st[(h + 1) % 3 if a == 1 else h % 3]

        tok = "(t p) d -> p t d"
        by_half = "(f p) n -> p f n"
        EARLY = [(wq_sb[:], wq.rearrange(by_half, p=P)), (bqk_sb[:], bqk), (wk_sb[:], wk.rearrange(by_half, p=P)),
                 (wi_sb[:], wi.rearrange(by_half, p=P)), (bi_sb[:], bi), (wv_sb[:], wv.rearrange(by_half, p=P)),
                 (bv_sb[:], bv.partition_broadcast(P))]
        LATE = [(stk["k1"][i][MROW:CROW], count_k[0:PARTS]) for i in range(2)]
        LATE += [(bo_sb[:], bo.partition_broadcast(P)), (wo_sb[:], wo.rearrange(by_half, p=P)),
                 (rk_sb[:], rope_k.rearrange("c (t p) d -> p c t d", p=P)),
                 (rq_sb[:], rope_q.rearrange("c (t p) d -> p c t d", p=P)),
                 (wgh_sb[:], wgh.rearrange(by_half, p=P)), (wb_sb[:], wb)]
        for i in range(2):
            LATE += [(stk["q2"][i][CROW:ROWS[2]], count_q), (stk["k2"][i][MROW:ROWS[2]], count_k)]

        block = stack.enter_context(nc.Block())

        @block.sync
        def _(sp):
            def load_x(b, par):
                if some(1, b - 2, 1):
                    sp.wait_ge(xb_done, count(1, b - 2, 1))
                sp.sem_inc(sp_ready, 1)
                if some(1, b - 1, 1):
                    sp.wait_ge(ln_done[1], count(1, b - 1, 1))
                sp.sem_inc(sp_ready, 1)
                sp.dma_start(x_in[par][:], x[b].rearrange(tok, p=P)).then_inc(x_loaded, 16)
                if first(b):
                    for dst, src in EARLY:
                        sp.dma_start(dst, src).then_inc(loaded_early, 16)
                    for dst, src in LATE:
                        sp.dma_start(dst, src).then_inc(loaded_late, 16)

            def load_ctx(b, par):
                if some(1, b - 1, 1):
                    sp.wait_ge(rot_done["k2"], count(1, b - 1, 1))
                if some(1, b - 1, 1):
                    sp.wait_ge(v_done[2], count(1, b - 1, 1))
                sp.sem_inc(sp_ready, 1)
                sp.dma_start(ctx_t[:], ctx_in_dram[b].rearrange(tok, p=P)).then_inc(ctx_loaded, 16)

            def stack_write(b, par, t):
                if some(16 * len(RUNS[t]), b, 0):
                    sp.wait_ge(stk_done[t], count(16 * len(RUNS[t]), b, 0))
                sp.wait_ge(low_done[t], count(2, b, 2))
                for f in range(HALVES):
                    sp.dma_start(scr[t][f].rearrange("r p s -> p r s"), parts[t][:, f]).then_inc(scr_done[t], 16)

            def stack_read(b, par, t):
                a = int(t[1])
                if some(UNITS, b - 1, 0):
                    sp.wait_ge(st_ready[a], count(HEADS, b - 1, 0))
                sp.wait_ge(scr_done[t], count(16 * HALVES, b, 16 * HALVES))
                rows = scr[t].rearrange("f r (d g) s -> f (r d) (g s)", d=DH)
                for blk, n, part in RUNS[t]:
                    dst = stk[t][par][blk * DH:(blk + n) * DH].rearrange("p (f g) s -> p f (g s)", f=HALVES)
                    sp.dma_start(dst, rows[:, part * DH:(part + n) * DH].rearrange("f r s -> r f s"))\
                      .then_inc(stk_done[t], 16)

            def m_turn(b, par, a, g):
                sp.wait_ge(m_out[a], count(2, b, g + 1))
                sp.dma_start(m_scr[a][g], m_rows[a][g][:]).then_inc(m_written[a][g], 16)

            def m_load(b, par, a, g):
                sp.wait_ge(m_written[a][g], count(16, b, 16))
                sp.dma_start(stk[f"q{a}"][par][MROW:MROW + PARTS, 8 * g:8 * g + 8, :],
                             m_scr[a][g].rearrange("(r h) s -> r h s", r=PARTS)).then_inc(m_done[a][g], 16)

            def hold(b, par):
                if some(2, b - 1, 0):
                    sp.wait_ge(x2_done, count(1, b - 1, 0))
                sp.wait_ge(x1_done, count(1, b, 1))
                sp.dma_start(x1_held[par][:], x1[par][:]).then_inc(held, 16)

            def experts_out(b, par):
                sp.wait_ge(y_done, count(1, b, 1))
                sp.sem_inc(sp_ready, 1)
                sp.dma_start(out[b].rearrange(tok, p=P), y[:]).then_inc(stored, 16)

            iterate(sp, dict(load_x=load_x, load_ctx=load_ctx, stack_write=stack_write, stack_read=stack_read,
                             m_turn=m_turn, m_load=m_load, hold=hold, experts_out=experts_out))
            sp.wait_ge(stored, 16 * BATCH)
            for t in RUNS:
                sp.wait_ge(scr_done[t], 16 * HALVES * BATCH)
            for a in (1, 2):
                for g in range(2):
                    sp.wait_ge(m_written[a][g], 16 * BATCH)

        @block.gpsimd
        def _(pool):
            for t in (ident, ident_b, causal_kq, causal_qk):
                pool.memset(t[:], 0.0).then_inc(zeroed, 1)
            pool.memset(eps_t[:], EPS)
            pool.memset(mhalf[:], -0.5)
            pool.memset(one_t[:], 1.0)
            for e in range(EXPERTS):
                pool.memset(eid[:, e:e + 1], float(e))
            pool.wait_ge(zeroed, 4)
            for t in (ident, ident_b):
                pool.affine_select(out=t[:], in_=t[:], compare_op=ALU.not_equal, fill=1.0, base=0,
                                   pattern=[[-1, P]], channel_multiplier=1)
            pool.affine_select(out=causal_kq[:], in_=causal_kq[:], compare_op=ALU.is_ge, fill=NEG, base=0,
                               pattern=[[0, 2], [1, P]], channel_multiplier=-1)
            pool.affine_select(out=causal_qk[:], in_=causal_qk[:], compare_op=ALU.is_ge, fill=NEG, base=0,
                               pattern=[[0, 2], [-1, P]], channel_multiplier=1).then_inc(consts, 1)
            for v in (*vals[1], *vals[2]):
                ins = pool.memset(v[:], 1.0)
            ins.then_inc(consts, 1)
            pool.wait_ge(consts, 2)

            def ln_stats(b, par, i):
                if some(1, b, 0):
                    pool.wait_ge(ln_done[i], count(1, b, 0))
                pool.wait_ge(ln_mv[i], count(1, b, 1))
                pool.tensor_tensor(var_eps[i][:], mv[i][:, :, 1], eps_t[:], ALU.add).then_inc(ln_rstd[i], 1)
                pool.wait_ge(ln_rstd[i], count(2, b, 1))
                pool.tensor_tensor(rstd[i][:], var_eps[i][:], mhalf[:], ALU.pow).then_inc(ln_rstd[i], 1)

            def x_bias(b, par):
                if some(1, b - 2, 1):
                    pool.wait_ge(x1_done, count(1, b - 2, 1))
                if first(b):
                    pool.wait_ge(loaded_late, 16 * len(LATE))
                pool.wait_ge(x_loaded, count(16, b, 16))
                pool.tensor_tensor(xb[par][:], x_in[par][:], bo_sb[:].unsqueeze(1).broadcast_to([P, TT, DIM]),
                                   ALU.add).then_inc(xb_done, 1)

            def split_low(b, par, t):
                if some(16 * HALVES, b, 0):
                    pool.wait_ge(scr_done[t], count(16 * HALVES, b, 0))
                pool.wait_ge(rest_done[t], count(1, b, 1))
                pool.tensor_tensor(parts[t][:, :, 1, :], rest[t][:],
                                   one_t[:].unsqueeze(2).broadcast_to([P, HALVES, SEQ]), ALU.mult).then_inc(low_done[t], 1)
                pool.wait_ge(low_done[t], count(2, b, 1))
                pool.tensor_tensor(parts[t][:, :, 2, :], rest[t][:], parts[t][:, :, 1, :], ALU.subtract)\
                    .then_inc(low_done[t], 1)

            def m_split(b, par, a, g):
                src, dst = neg_max[a][:, :, 8 * g:8 * g + 8], m_parts[a][g]
                one = one_t[:].unsqueeze(2).broadcast_to([P, TT, 8])
                if some(2, b - 1, g + 1):
                    pool.wait_ge(m_raw[a], count(2, b - 1, g + 1))
                pool.wait_ge(mx_done[a], count(HEADS, b, 8 * g + 8))
                pool.tensor_tensor(dst[:, :, 0:8], src, one, ALU.mult).then_inc(m_step[a], 1)
                pool.wait_ge(m_step[a], count(8, b, 4 * g + 1))
                pool.tensor_tensor(m_rest[a][:], src, dst[:, :, 0:8], ALU.subtract).then_inc(m_step[a], 1)
                pool.wait_ge(m_step[a], count(8, b, 4 * g + 2))
                pool.tensor_tensor(dst[:, :, 8:16], m_rest[a][:], one, ALU.mult).then_inc(m_step[a], 1)
                pool.wait_ge(m_step[a], count(8, b, 4 * g + 3))
                pool.tensor_tensor(dst[:, :, 16:24], m_rest[a][:], dst[:, :, 8:16], ALU.subtract)\
                    .then_inc(m_step[a], 1)

            def x_residual(b, par):
                pool.wait_ge(held, count(16, b, 16))
                if some(1, b - 1, 1):
                    pool.wait_ge(y_done, count(1, b - 1, 1))
                pool.wait_ge(o_done[2], count(2, b, 2))
                pool.tensor_tensor(x2[:], x1_held[par][:], o[2][:], ALU.add).then_inc(x2_done, 1)

            def swapped(t, src, table):
                s = src[:].rearrange("p t (i e) -> p t i e", e=2)
                d = rot_b[t][:].rearrange("p t (i e) -> p t i e", e=2)
                w = table[:, 1].rearrange("p t (i e) -> p t i e", e=2)
                pool.tensor_tensor(d[:, :, :, 0], s[:, :, :, 1], w[:, :, :, 0], ALU.mult)
                pool.tensor_tensor(d[:, :, :, 1], s[:, :, :, 0], w[:, :, :, 1], ALU.mult).then_inc(rb_done[t], 1)

            def rotation_sum(t):
                lie = "p t (f g d) -> p (t f) g d"
                pool.tensor_tensor(rotated[t][:].rearrange("p t (f d g) -> p (t f) g d", f=HALVES, d=DH),
                                   rot_a[t][:].rearrange(lie, f=HALVES, d=DH),
                                   rot_b[t][:].rearrange(lie, f=HALVES, d=DH), ALU.add).then_inc(rot_done[t], 1)

            def rotate_k(b, par):
                pool.wait_ge(ctx_loaded, count(16, b, 16))
                pool.tensor_tensor(rot_a["k2"][:], ctx_t[:], rk_sb[:, 0], ALU.mult).then_inc(ra_done["k2"], 1)
                swapped("k2", ctx_t, rk_sb)
                if some(1, b, 0):
                    pool.wait_ge(raw_ready["k2"], count(1, b, 0))
                pool.wait_ge(ra_done["k2"], count(1, b, 1))
                pool.wait_ge(rb_done["k2"], count(1, b, 1))
                rotation_sum("k2")

            def rotate_q(b, par):
                pool.wait_ge(ln_done[2], count(1, b, 1))
                pool.tensor_tensor(rot_a["q2"][:], xn[2][:], rq_sb[:, 0], ALU.mult).then_inc(ra_done["q2"], 1)
                swapped("q2", xn[2], rq_sb)
                if some(1, b, 0):
                    pool.wait_ge(raw_ready["q2"], count(1, b, 0))
                pool.wait_ge(ra_done["q2"], count(1, b, 1))
                pool.wait_ge(rb_done["q2"], count(1, b, 1))
                rotation_sum("q2")

            iterate(pool, dict(ln_stats=ln_stats, x_bias=x_bias, m_split=m_split, x_residual=x_residual,
                               split_low=split_low, rotate_k=rotate_k,
                               rotate_q=rotate_q))

        @block.scalar
        def _(act):
            act.wait_ge(consts, 2)

            def scores(b, par, a, u):
                if u >= 4:
                    act.wait_ge(pv_ready[a], count(GROUPS, b, u // 2 - 1))
                elif a == 1:
                    if some(GROUPS, b - 2, u // 2 - 1):
                        act.wait_ge(pv_ready[2], count(GROUPS, b - 2, u // 2 - 1))
                elif some(GROUPS, b + 3, u // 2 - 1):
                    act.wait_ge(pv_ready[1], count(GROUPS, b + 3, u // 2 - 1))
                for h in range(2 * u, 2 * u + 2):
                    act.wait_ge(st_ready[a], count(HEADS, b, h + 1))
                    act.activation(expo[u % 4][:, h % 2, 0:WIDTH[a]], st_of(a, h)[:, 0:WIDTH[a]], ACT.Exp, scale=SCALE)\
                       .then_inc(exp_done[a], 1)

            def values(b, par, a, g):
                act.wait_ge(pv_ready[a], count(GROUPS, b, g + 1))
                act.activation(oT[a][:, g, :], pv[:, g % 2, :], ACT.Copy).then_inc(pv_done[a], 1)

            def m_turn(b, par, a, g):
                misc = misc_of("m_turn", a, g)
                if some(16, b, 0):
                    act.wait_ge(m_written[a][g], count(16, b, 0))
                act.wait_ge(m_raw[a], count(2, b, g + 1))
                act.activation(m_rows[a][g][:], misc[0:PARTS * 8, 0:P].bitcast(BF16), ACT.Copy).then_inc(m_out[a], 1)

            def xn_turn(b, par, i):
                misc = misc_of("xn_turn", i)
                act.wait_ge(turned[i], count(1, b, 1))
                act.activation(xnT[i][:].rearrange("p f s -> p (f s)"), misc[:], ACT.Copy).then_inc(turned_out[i], 1)

            def high(b, t):
                misc = misc_of("project", t) if t[1] == "1" else misc_of(t + "_turn")
                if some(16 * HALVES, b, 0):
                    act.wait_ge(scr_done[t], count(16 * HALVES, b, 0))
                if first(b) and t == "q1":
                    act.wait_ge(loaded_early, 16 * len(EARLY))
                act.wait_ge(raw_ready[t], count(1, b, 1))
                for f in range(HALVES):
                    src = misc[:, f * SEQ:(f + 1) * SEQ]
                    if t[1] == "1":
                        c = f + (2 if t == "k1" else 0)
                        i = act.activation(parts[t][:, f, 0, :], src, ACT.Identity, bias=bqk_sb[:, c:c + 1])
                    else:
                        i = act.activation(parts[t][:, f, 0, :], src, ACT.Copy)
                i.then_inc(high_done[t], 1)

            def idx_project(b, par):
                misc = misc_of("idx_project")
                act.wait_ge(ip_raw, count(1, b, 1))
                act.activation(idxT[:, 0:SEQ], misc[0:IDX, 0:SEQ], ACT.Identity, bias=bi_sb[:, 0:1])
                act.activation(idxT[:, SEQ:SEQ + ASSOC], misc[0:IDX, SEQ:SEQ + ASSOC], ACT.Identity,
                               bias=bi_sb[:, 1:2]).then_inc(ip_done, 1)

            def idx_scores(b, par):
                misc = misc_of("idx_scores")
                if some(1, b, 0):
                    act.wait_ge(mask_done, count(1, b, 0))
                act.wait_ge(is_raw, count(1, b, 1))
                act.activation(work[:].rearrange("p t k -> p (t k)"), misc[:, 0:TT * ASSOC], ACT.Relu)\
                   .then_inc(is_done, 1)

            def mask_turn(b, par):
                misc = misc_of("mask_turn")
                act.wait_ge(maskT_raw, count(1, b, 1))
                act.activation(maskT[:], misc[:, 0:P].bitcast(BF16), ACT.Copy).then_inc(maskT_done, 1)

            def o_features(b, par):
                misc = misc_of("o_features")
                act.wait_ge(of_raw, count(1, b, 1))
                act.activation(o1T[:].rearrange("p f s -> p (f s)"), misc[:], ACT.Copy).then_inc(of_done, 1)

            def ctx_values(b, par):
                if some(GROUPS, b - 1, 0):
                    act.wait_ge(pv_ready[2], count(GROUPS, b - 1, 0))
                act.wait_ge(ctx_loaded, count(16, b, 16))
                for t in range(TT):
                    i = act.activation(vals[2][par][:, t, :, 0:DH], ctx_t[:, t, :].rearrange("p (h d) -> p h d", d=DH),
                                       ACT.Copy)
                i.then_inc(v_done[2], 1)

            def gate(b, par):
                act.wait_ge(g_step, count(G_STEPS, b, 2))
                act.activation(gexp[:], gap[:], ACT.Exp).then_inc(g_exp, 1)

            def experts_in(b, par):
                misc = misc_of("experts_in")
                if some(G_STEPS, b, 0):
                    act.wait_ge(g_step, count(G_STEPS, b, 0))
                act.wait_ge(gh_raw, count(1, b, 1))
                src = misc[:, 0:TT * 136].rearrange("p (t c) -> p t c", t=TT)
                act.activation(hid[:], src[:, :, 0:P], ACT.Copy)
                act.activation(logits[:], src[:, :, P:P + EXPERTS], ACT.Copy).then_inc(gh_done, 1)

            def h_turn(b, par):
                misc = misc_of("h_turn")
                act.wait_ge(ht_raw, count(1, b, 1))
                act.activation(hT[:], misc[:, 0:SEQ], ACT.Copy).then_inc(ht_done, 1)

            iterate(act, dict(scores=scores, values=values, m_turn=m_turn, xn_turn=xn_turn,
                              project=lambda b, par, t: high(b, t), k2_turn=lambda b, par: high(b, "k2"),
                              q2_turn=lambda b, par: high(b, "q2"), idx_project=idx_project, idx_scores=idx_scores,
                              mask_turn=mask_turn, o_features=o_features, ctx_values=ctx_values, gate=gate,
                              experts_in=experts_in, h_turn=h_turn))

        @block.vector
        def _(dve):
            LN_IN = {1: lambda par: x_in[par], 2: lambda par: x1[par], 3: lambda par: x2}

            def maxima(b, par, a, u):
                for h in range(2 * u, 2 * u + 2):
                    dve.wait_ge(mx_ready[a], count(HEADS, b, h + 1))
                    src = mx[h % 2]
                    if a == 1:
                        i = dve.tensor_reduce(neg_max[a][:, :, h], src[:].rearrange("p (t k) -> p t k", t=TT), AX.X,
                                              ALU.max, negate=True)
                    else:
                        dve.tensor_reduce(neg_max[a][:, 0, h:h + 1], src[:, 0:P], AX.X, ALU.max, negate=True)
                        i = dve.tensor_reduce(neg_max[a][:, 1, h:h + 1], src[:, P:3 * P], AX.X, ALU.max, negate=True)
                    i.then_inc(mx_done[a], 1)

            def topk(b, par, r):
                if r == 0:
                    dve.wait_ge(is_done, count(1, b, 1))
                    dve.memset(held_back[:], 0.0)
                for t in range(TT):
                    if r > 0:
                        dve.wait_ge(topk_step, 4 * r - 1 + t)
                    dve.max(max8[:, t, :], work[:, t, :]).then_inc(topk_step, 1)
                for t in range(TT):
                    dve.wait_ge(topk_step, 4 * r + 1 + t)
                    dve.match_replace(work[:, t, :], max8[:, t, :], work[:, t, :], -1.0).then_inc(topk_step, 1)
                if r == 7:
                    dve.wait_ge(topk_step, 32)
                    dve.sem_clear(topk_step)
                    if some(UNITS, b, 0):
                        dve.wait_ge(mx_ready[1], count(HEADS, b, 0))
                    if some(1, b, 0):
                        dve.wait_ge(maskT_raw, count(1, b, 0))
                    dve.tensor_scalar(mask[:], work[:], 0.0, NEG, ALU.is_ge, ALU.mult).then_inc(mask_done, 1)

            def ln_stats(b, par, i):
                src = LN_IN[i](par)
                if i == 1:
                    dve.wait_ge(x_loaded, count(16, b, 16))
                if i == 2:
                    dve.wait_ge(x1_done, count(1, b, 1))
                if i == 3:
                    dve.wait_ge(x2_done, count(1, b, 1))
                if some(2, b, 0):
                    dve.wait_ge(ln_rstd[i], count(2, b, 0))
                for t in range(TT):
                    ins = dve.bn_stats(stats[i][:, t, :], src[:, t, :])
                ins.then_inc(ln_bn, 1)
                dve.wait_ge(ln_bn, 1)
                dve.sem_clear(ln_bn)
                for t in range(TT):
                    ins = dve.bn_aggr(mv[i][:, t, :], stats[i][:, t, :])
                ins.then_inc(ln_mv[i], 1)

            def ln_apply(b, par, i):
                src = LN_IN[i](par)
                if i in turned:
                    if some(1, b, 0):
                        dve.wait_ge(turned[i], count(1, b, 0))
                else:
                    if some(1, b, 0):
                        dve.wait_ge(rot_done["q2"], count(1, b, 0))
                dve.wait_ge(ln_mv[i], count(1, b, 1))
                dve.wait_ge(ln_rstd[i], count(2, b, 2))
                for t in range(TT):
                    ins = dve.tensor_scalar(xn[i][:, t, :], src[:, t, :], mv[i][:, t, 0:1], rstd[i][:, t:t + 1],
                                            ALU.subtract, ALU.mult)
                ins.then_inc(ln_done[i], 1)

            def split_rest(b, par, t):
                misc = misc_of("project", t) if t[1] == "1" else misc_of(t + "_turn")
                if some(2, b, 0):
                    dve.wait_ge(low_done[t], count(2, b, 0))
                if first(b) and t == "q1":
                    dve.wait_ge(loaded_early, 16 * len(EARLY))
                    dve.wait_ge(consts, 2)
                dve.wait_ge(raw_ready[t], count(1, b, 1))
                dve.wait_ge(high_done[t], count(1, b, 1))
                if t[1] == "1":
                    for f in range(HALVES):
                        c = f + (2 if t == "k1" else 0)
                        i = dve.scalar_tensor_tensor(out=rest[t][:, f, :], in0=misc[:, f * SEQ:(f + 1) * SEQ],
                                                     scalar=bqk_sb[:, c:c + 1], in1=parts[t][:, f, 0, :],
                                                     op0=ALU.add, op1=ALU.subtract)
                else:
                    i = dve.tensor_tensor(rest[t][:], misc[:].rearrange("p (f s) -> p f s", f=HALVES),
                                          parts[t][:, :, 0, :], ALU.subtract)
                i.then_inc(rest_done[t], 1)

            def project_v(b, par):
                misc = misc_of("project_v")
                if some(GROUPS, b - 1, 0):
                    dve.wait_ge(pv_ready[1], count(GROUPS, b - 1, 0))
                dve.wait_ge(v_raw, count(1, b, 1))
                for t in range(TT):
                    i = dve.tensor_tensor(vals[1][par][:, t, :, 0:DH],
                                          misc[:, t * DIM:(t + 1) * DIM].rearrange("p (h d) -> p h d", d=DH),
                                          bv_sb[:].rearrange("p (h d) -> p h d", d=DH), ALU.add)
                i.then_inc(v_done[1], 1)

            def o_turn(b, par, a, t):
                misc = misc_of("o_turn", a, t)
                src = misc[:].rearrange("p (h c) -> p h c", c=32)
                dve.wait_ge(o_raw[a], count(2, b, t + 1))
                if a == 2 and some(1, b, 0):
                    dve.wait_ge(x2_done, count(1, b, 0))
                dve.reciprocal(rsum[a][:, t, :], src[:, :, DH]).then_inc(o_rcp[a], 1)
                dve.wait_ge(o_rcp[a], count(2, b, t + 1))
                dst = o[a][:, t, :].rearrange("p (h d) -> p h d", d=DH)
                dve.tensor_tensor(dst, src[:, :, 0:DH], rsum[a][:, t, :].unsqueeze(2).broadcast_to([P, HEADS, DH]),
                                  ALU.mult).then_inc(o_done[a], 1)

            def out_proj(b, par):
                misc = misc_of("out_proj")
                if some(16, b - 1, 0):
                    dve.wait_ge(held, count(16, b - 1, 0))
                dve.wait_ge(xb_done, count(1, b, 1))
                dve.wait_ge(wo_raw, count(1, b, 1))
                dve.tensor_tensor(x1[par][:], misc[:].rearrange("p (t d) -> p t d", t=TT), xb[par][:], ALU.add)\
                   .then_inc(x1_done, 1)

            def gate(b, par):
                dve.wait_ge(gh_done, count(1, b, 1))
                dve.memset(held_back[:], 0.0)
                for t in range(TT):
                    i = dve.max(top8[:, t, :], logits[:, t, :])
                i.then_inc(g_max, 1)
                dve.wait_ge(g_max, 1)
                dve.sem_clear(g_max)
                for t in range(TT):
                    i = dve.max_index(top_i[:, t, :], top8[:, t, :], logits[:, t, :])
                i.then_inc(g_step, 1)
                dve.tensor_tensor(gap[:], top8[:, :, 1], top8[:, :, 0], ALU.subtract).then_inc(g_step, 1)
                dve.wait_ge(g_step, count(G_STEPS, b, 1))
                dve.tensor_copy(top_f[:], top_i[:, :, 0:2]).then_inc(g_step, 1)

            def gate_weights(b, par):
                dve.wait_ge(g_exp, count(1, b, 1))
                dve.tensor_scalar(gden[:], gexp[:], 1.0, None, ALU.add).then_inc(g_step, 1)
                dve.wait_ge(g_step, count(G_STEPS, b, 4))
                dve.reciprocal(w_top[:, 0, :], gden[:]).then_inc(g_step, 1)
                dve.wait_ge(g_step, count(G_STEPS, b, 5))
                dve.tensor_tensor(w_top[:, 1, :], gexp[:], w_top[:, 0, :], ALU.mult).then_inc(g_step, 1)
                dve.wait_ge(g_step, count(G_STEPS, b, 6))
                for k in range(2):
                    for t in range(TT):
                        i = dve.tensor_scalar(gw[:, k, t, :], eid[:], top_f[:, t, k:k + 1], w_top[:, k, t:t + 1],
                                              ALU.is_equal, ALU.mult)
                i.then_inc(g_step, 1)
                dve.wait_ge(g_step, count(G_STEPS, b, 7))
                dve.tensor_tensor(cw[:], gw[:, 0], gw[:, 1], ALU.add).then_inc(g_step, 1)
                if some(1, b, 0):
                    dve.wait_ge(ht_raw, count(1, b, 0))
                dve.wait_ge(g_step, count(G_STEPS, b, 8))
                for t in range(TT):
                    i = dve.tensor_tensor(hidw[:, t, :].rearrange("p (e r) -> p e r", e=EXPERTS),
                                          hid[:, t, :].rearrange("p (e r) -> p e r", e=EXPERTS),
                                          cw[:, t, :].unsqueeze(2).broadcast_to([P, EXPERTS, RANK]), ALU.mult)
                i.then_inc(g_step, 1)

            def experts_out(b, par):
                misc = misc_of("experts_out")
                if some(16, b, 0):
                    dve.wait_ge(stored, count(16, b, 0))
                dve.wait_ge(fo_raw, count(1, b, 1))
                dve.tensor_tensor(y[:], misc[:].rearrange("p (t d) -> p t d", t=TT), x2[:], ALU.add)\
                   .then_inc(y_done, 1)

            iterate(dve, dict(maxima=maxima, topk=topk, ln_stats=ln_stats, ln_apply=ln_apply,
                              split_rest=split_rest,
                              project_v=project_v, o_turn=o_turn, out_proj=out_proj, gate=gate,
                              gate_weights=gate_weights, experts_out=experts_out))

        @block.tensor
        def _(pe):
            pe.wait_ge(consts, 1)
            taken = {}

            def misc_carry(n):
                if not isinstance(n, int) or n == LOOP + 2 * TRIPS:
                    taken[misc_of("project_v").name] = (v_done[1], count(1, n, 1))
                    taken[misc_of("experts_out").name] = (y_done, count(1, n - 5, 1))

            def two_diagonals(tile):
                return tile[:].rearrange("p (t c) -> p t c", t=2)[:, :, 0:P]

            def scores(b, par, a, u):
                if u == 0 and a == 1:
                    pe.wait_ge(maskT_done, count(1, b, 1))
                if u == 0 and some(HEADS, b, 0):
                    pe.wait_ge(exp_done[a], count(HEADS, b, 0))
                if u % 4 == 0:
                    pe.wait_ge(m_done[a][u // 4], count(16, b, 16))
                q, k, rows = stk[f"q{a}"][par], stk[f"k{a}"][par], ROWS[a]
                for h in range(2 * u, 2 * u + 2):
                    dst = st_of(a, h)
                    if h >= 3:
                        pe.wait_ge(exp_done[a], count(HEADS, b, h - 2))
                    elif a == 1 and some(HEADS, b - 3, 14 + h):
                        pe.wait_ge(exp_done[2], count(HEADS, b - 3, 14 + h))
                    elif a == 2:
                        pe.wait_ge(exp_done[1], count(HEADS, b + 2, (15, 16, 14)[h]))
                    pe.matmul(dst[:, 0:SEQ], k[0:rows, h, 0:P], q[0:rows, h, :], start=True, stop=False)
                    if a == 1:
                        pe.matmul(dst[:, 0:SEQ], ident_b[:], maskT[:], start=False, stop=True)
                        i = pe.matmul(dst[:, SEQ:2 * SEQ], k[0:rows, h, P:SEQ], q[0:rows, h, :],
                                      start=True, stop=True)
                    else:
                        pe.matmul(dst[:, SEQ:SEQ + P], k[0:rows, h, P:SEQ], q[0:rows, h, P:SEQ],
                                  start=False, stop=False)
                        i = pe.matmul(two_diagonals(dst), ident_b[:], causal_kq[:], start=False, stop=True)
                    i.then_inc(st_ready[a], 1)

            def maxima(b, par, a, u):
                if first(b) and a == 1 and u == 0:
                    pe.wait_ge(loaded_late, 16 * len(LATE))
                if u == 0:
                    for t in (f"q{a}", f"k{a}"):
                        pe.wait_ge(stk_done[t], count(16 * len(RUNS[t]), b, 16 * len(RUNS[t])))
                    if a == 1:
                        pe.wait_ge(mask_done, count(1, b, 1))
                    if some(HEADS, b, 0):
                        pe.wait_ge(mx_done[a], count(HEADS, b, 0))
                q, k = stk[f"q{a}"][par], stk[f"k{a}"][par]
                for h in range(2 * u, 2 * u + 2):
                    dst = mx[h % 2]
                    if h >= 2:
                        pe.wait_ge(mx_done[a], count(HEADS, b, h - 1))
                    elif a == 2:
                        pe.wait_ge(mx_done[1], count(HEADS, b + 2, 15 + h))
                    elif some(HEADS, b - 3, 15 + h):
                        pe.wait_ge(mx_done[2], count(HEADS, b - 3, 15 + h))
                    if a == 1:
                        for t in range(TT):
                            pe.matmul(dst[:, t * SEQ:(t + 1) * SEQ], q[0:PROD, h, t * P:(t + 1) * P],
                                      k[0:PROD, h, :], start=(t == 0), stop=False)
                        i = pe.matmul(two_diagonals(dst), ident_b[:], mask[:], start=False, stop=True)
                    else:
                        pe.matmul(dst[:, 0:P], q[0:PROD, h, 0:P], k[0:PROD, h, 0:P], start=True, stop=False)
                        pe.matmul(dst[:, P:3 * P], q[0:PROD, h, P:SEQ], k[0:PROD, h, :], start=False, stop=False)
                        i = pe.matmul(two_diagonals(dst), ident_b[:], causal_qk[:], start=False, stop=True)
                    i.then_inc(mx_ready[a], 1)

            def values(b, par, a, g):
                if g == 0:
                    pe.wait_ge(v_done[a], count(1, b, 1))
                pe.wait_ge(exp_done[a], count(HEADS, b, 4 * g + 4))
                if g >= 2:
                    pe.wait_ge(pv_done[a], count(GROUPS, b, g - 1))
                elif a == 1:
                    if some(GROUPS, b - 2, g - 1):
                        pe.wait_ge(pv_done[2], count(GROUPS, b - 2, g - 1))
                elif some(GROUPS, b + 3, g - 1):
                    pe.wait_ge(pv_done[1], count(GROUPS, b + 3, g - 1))
                for kt in range(TT):
                    for c in range(4):
                        h, src = 4 * g + c, expo[(2 * g + c // 2) % 4]
                        q0 = P * kt if a == 2 else 0
                        i = pe.matmul(pv[32 * c:32 * c + 32, g % 2, q0:SEQ], vals[a][par][:, kt, h, :],
                                      src[:, c % 2, kt * SEQ:kt * SEQ + SEQ - q0], start=(kt == 0), stop=(kt == 1))
                i.then_inc(pv_ready[a], 1)

            def m_turn(b, par, a, g):
                misc = misc_of("m_turn", a, g)
                if misc.name in taken:
                    pe.wait_ge(*taken[misc.name])
                pe.wait_ge(m_step[a], count(8, b, 4 * g + 4))
                for t in range(TT):
                    i = pe.transpose(misc[:, 0:P].bitcast(BF16)[0:PARTS * 8, t * P:(t + 1) * P],
                                 m_parts[a][g][:, t, :], ident_b[:])
                i.then_inc(m_raw[a], 1)
                taken[misc.name] = (m_out[a], count(2, b, g + 1))

            def turn(misc, src):
                for f in range(HALVES):
                    for t in range(TT):
                        i = pe.transpose(misc[:, f * SEQ + t * P:f * SEQ + (t + 1) * P],
                                         src[:, t, f * P:(f + 1) * P], ident[:])
                return i

            def xn_turn(b, par, i):
                misc = misc_of("xn_turn", i)
                if misc.name in taken:
                    pe.wait_ge(*taken[misc.name])
                pe.wait_ge(ln_done[i], count(1, b, 1))
                turn(misc, xn[i]).then_inc(turned[i], 1)
                taken[misc.name] = (turned_out[i], count(1, b, 1))

            def project(b, par, t):
                misc = misc_of("project", t)
                w = wq_sb if t == "q1" else wk_sb
                if misc.name in taken:
                    pe.wait_ge(*taken[misc.name])
                if first(b) and t == "q1":
                    pe.wait_ge(loaded_early, 16 * len(EARLY))
                pe.wait_ge(turned_out[1], count(1, b, 1))
                for f in range(HALVES):
                    for c in range(HALVES):
                        i = pe.matmul(misc[:, f * SEQ:(f + 1) * SEQ], w[:, c, f * P:(f + 1) * P], xnT[1][:, c, :],
                                      start=(c == 0), stop=(c == 1))
                i.then_inc(raw_ready[t], 1)
                taken[misc.name] = (rest_done[t], count(1, b, 1))

            def project_v(b, par):
                misc = misc_of("project_v")
                if misc.name in taken:
                    pe.wait_ge(*taken[misc.name])
                for t in range(TT):
                    for c in range(HALVES):
                        i = pe.matmul(misc[:, t * DIM:(t + 1) * DIM], xnT[1][:, c, t * P:(t + 1) * P], wv_sb[:, c, :],
                                      start=(c == 0), stop=(c == 1))
                i.then_inc(v_raw, 1)
                taken[misc.name] = (v_done[1], count(1, b, 1))

            def idx_project(b, par):
                misc = misc_of("idx_project")
                if misc.name in taken:
                    pe.wait_ge(*taken[misc.name])
                for k, n in ((0, SEQ), (1, ASSOC)):
                    for c in range(HALVES):
                        i = pe.matmul(misc[0:IDX, k * SEQ:k * SEQ + n], wi_sb[:, c, k * IDX:(k + 1) * IDX],
                                      xnT[1][:, c, 0:n], start=(c == 0), stop=(c == 1))
                i.then_inc(ip_raw, 1)
                taken[misc.name] = (ip_done, count(1, b, 1))

            def idx_scores(b, par):
                misc = misc_of("idx_scores")
                if misc.name in taken:
                    pe.wait_ge(*taken[misc.name])
                pe.wait_ge(ip_done, count(1, b, 1))
                for t in range(TT):
                    i = pe.matmul(misc[:, t * ASSOC:(t + 1) * ASSOC], idxT[:, t * P:(t + 1) * P],
                                  idxT[:, SEQ:SEQ + ASSOC], start=True, stop=True)
                i.then_inc(is_raw, 1)
                taken[misc.name] = (is_done, count(1, b, 1))

            def mask_turn(b, par):
                misc = misc_of("mask_turn")
                if misc.name in taken:
                    pe.wait_ge(*taken[misc.name])
                pe.wait_ge(mask_done, count(1, b, 1))
                for t in range(TT):
                    i = pe.transpose(misc[:, 0:P].bitcast(BF16)[:, t * P:(t + 1) * P], mask[:, t, :], ident_b[:])
                i.then_inc(maskT_raw, 1)
                taken[misc.name] = (maskT_done, count(1, b, 1))

            def o_turn(b, par, a, t):
                misc = misc_of("o_turn", a, t)
                if misc.name in taken:
                    pe.wait_ge(*taken[misc.name])
                pe.wait_ge(pv_done[a], count(GROUPS, b, GROUPS))
                for g in range(GROUPS):
                    i = pe.transpose(misc[:, g * P:(g + 1) * P], oT[a][:, g, t * P:(t + 1) * P], ident[:])
                i.then_inc(o_raw[a], 1)
                taken[misc.name] = (o_done[a], count(2, b, t + 1))

            def o_features(b, par):
                misc = misc_of("o_features")
                if misc.name in taken:
                    pe.wait_ge(*taken[misc.name])
                pe.wait_ge(o_done[1], count(2, b, 2))
                turn(misc, o[1]).then_inc(of_raw, 1)
                taken[misc.name] = (of_done, count(1, b, 1))

            def out_proj(b, par):
                misc = misc_of("out_proj")
                if misc.name in taken:
                    pe.wait_ge(*taken[misc.name])
                pe.wait_ge(of_done, count(1, b, 1))
                for t in range(TT):
                    for c in range(HALVES):
                        i = pe.matmul(misc[:, t * DIM:(t + 1) * DIM], o1T[:, c, t * P:(t + 1) * P], wo_sb[:, c, :],
                                      start=(c == 0), stop=(c == 1))
                i.then_inc(wo_raw, 1)
                taken[misc.name] = (x1_done, count(1, b, 1))

            def rotated_turn(b, t):
                misc = misc_of(t + "_turn")
                if misc.name in taken:
                    pe.wait_ge(*taken[misc.name])
                pe.wait_ge(rot_done[t], count(1, b, 1))
                turn(misc, rotated[t]).then_inc(raw_ready[t], 1)
                taken[misc.name] = (rest_done[t], count(1, b, 1))

            def experts_in(b, par):
                misc = misc_of("experts_in")
                if misc.name in taken:
                    pe.wait_ge(*taken[misc.name])
                pe.wait_ge(turned_out[3], count(1, b, 1))
                for t in range(TT):
                    for c in range(HALVES):
                        i = pe.matmul(misc[:, t * 136:(t + 1) * 136], xnT[3][:, c, t * P:(t + 1) * P],
                                      wgh_sb[:, c, :], start=(c == 0), stop=(c == 1))
                i.then_inc(gh_raw, 1)
                taken[misc.name] = (gh_done, count(1, b, 1))

            def h_turn(b, par):
                misc = misc_of("h_turn")
                if misc.name in taken:
                    pe.wait_ge(*taken[misc.name])
                pe.wait_ge(g_step, count(G_STEPS, b, G_STEPS))
                for t in range(TT):
                    i = pe.transpose(misc[:, t * P:(t + 1) * P], hidw[:, t, :], ident[:])
                i.then_inc(ht_raw, 1)
                taken[misc.name] = (ht_done, count(1, b, 1))

            def experts_out(b, par):
                misc = misc_of("experts_out")
                if misc.name in taken:
                    pe.wait_ge(*taken[misc.name])
                pe.wait_ge(ht_done, count(1, b, 1))
                for t in range(TT):
                    i = pe.matmul(misc[:, t * DIM:(t + 1) * DIM], hT[:, t * P:(t + 1) * P], wb_sb[:],
                                  start=True, stop=True)
                i.then_inc(fo_raw, 1)
                taken[misc.name] = (y_done, count(1, b, 1))

            handlers = dict(misc_carry=misc_carry, scores=scores, maxima=maxima, values=values, m_turn=m_turn,
                            xn_turn=xn_turn, project=project, project_v=project_v, idx_project=idx_project, idx_scores=idx_scores,
                            mask_turn=mask_turn, o_turn=o_turn, o_features=o_features, out_proj=out_proj,
                            k2_turn=lambda b, par: rotated_turn(b, "k2"), q2_turn=lambda b, par: rotated_turn(b, "q2"),
                            experts_in=experts_in, h_turn=h_turn, experts_out=experts_out)

            iterate(pe, handlers)


_CONSTS = ("rope_q", "rope_k", "count_q", "count_k")
_INS = ["x", "ctx", "wq", "wk", "wv", "wo", "wi", "bqk", "bv", "bo", "bi", "wgh", "wb", *_CONSTS]


def constants():
    import numpy as np

    f = np.float32
    half = DH // 2
    scale_vec = (np.arange(0, DH, 2, dtype=f) + f(0.4 * DH)) / f(1.4 * DH)
    power = np.arange(-SEQ // 2, SEQ - SEQ // 2, dtype=f) / f(128)
    scale = scale_vec[None, :] ** power[:, None]
    inv_freq = f(1.0) / f(10000.0) ** (np.arange(half, dtype=f) / f(half))
    angle = np.arange(SEQ, dtype=f)[:, None] * inv_freq[None, :]
    tables = []
    for s in (scale, f(1.0) / scale):
        cos, sin = np.cos(angle) * s, np.sin(angle) * s
        c = np.tile(np.repeat(cos, 2, axis=1), (1, HEADS))
        signed = np.tile(np.stack([-sin, sin], axis=-1).reshape(SEQ, DH), (1, HEADS))
        tables.append(np.stack([c, signed]).astype(f))
    b16 = np.dtype("bfloat16")
    count_q = np.zeros((4, PARTS, HEADS, SEQ), b16)
    h, q = np.arange(HEADS)[:, None], np.arange(SEQ)[None, :]
    for i in range(4):
        n = np.ones((HEADS, SEQ))
        for r in (2, 4):
            j = h // (HEADS // r)
            n = n + ((q % r == j) & (i % r == j))
        left = np.log(n) / SCALE
        for part in range(PARTS):
            count_q[i, part] = left.astype(b16)
            left = left - count_q[i, part].astype(np.float64)
    count_k = np.ones((PARTS + 4 * PARTS, HEADS, SEQ), b16)
    for i in range(4):
        count_k[PARTS + PARTS * i:PARTS + PARTS * (i + 1)] = (np.arange(SEQ) % 4 == i).astype(b16)
    return tables[0], tables[1], count_q.reshape(4 * PARTS, HEADS, SEQ), count_k


def kernel(**inputs):
    import numpy as np
    import concourse.bacc as bacc
    from concourse.bass_utils import run_bass_kernel_spmd

    g = {k: np.asarray(v) for k, v in inputs.items()}
    order = np.arange(DIM).reshape(HALVES, HEADS // HALVES, DH).transpose(0, 2, 1).reshape(-1)
    a, f = "L0_attn_", "L0_ffn_"
    arrays = dict(
        x=g["x"], ctx=g["ctx_1024"], wq=g[a + "wq_w"][:, order], wk=g[a + "wk_w"][:, order], wv=g[a + "wv_w"],
        wo=g[a + "wo_w"], wi=np.concatenate([g[a + "wqi_w"], g[a + "wki_w"]], axis=1),
        bqk=np.concatenate([g[a + "wq_b"][order], g[a + "wk_b"][order]]).reshape(4, P).T, bv=g[a + "wv_b"], bo=g[a + "wo_b"],
        bi=np.stack([g[a + "wqi_b"], g[a + "wki_b"]], axis=1),
        wgh=np.concatenate([g[f + "A"].transpose(1, 0, 2).reshape(DIM, EXPERTS * RANK), g[f + "Wg"]], axis=1),
        wb=g[f + "B"].reshape(EXPERTS * RANK, DIM), **dict(zip(_CONSTS, constants())))
    arrays = {k: np.ascontiguousarray(v) for k, v in arrays.items()}
    nc = bacc.Bacc("TRN2", target_bir_lowering=False, num_devices=1)
    args = [nc.dram_tensor(f"in_{n}", arrays[n].shape, mybir.dt.from_np(arrays[n].dtype), kind="ExternalInput").ap()
            for n in _INS]
    args.append(nc.dram_tensor("out_0", (BATCH, SEQ, DIM), F32, kind="ExternalOutput").ap())
    decoder_layer(nc, *args)
    r = run_bass_kernel_spmd(nc, [{f"in_{n}": arrays[n] for n in _INS}], core_ids=[0])
    return r.results[0]["out_0"]
```
